# Optimizing a Trainium2 kernel written in Bass

```python
import numpy as np
import jax
import jax.numpy as jnp

def _softmax(x, axis=-1):
    return jax.nn.softmax(x, axis=axis)

def _gelu(x):
    return jax.nn.gelu(x, approximate=True)

def _silu(x):
    return jax.nn.silu(x)

def _sigmoid(x):
    return jax.nn.sigmoid(x)

def _layernorm(x, axis=-1, eps=1e-05):
    m = jnp.mean(x, axis=axis, keepdims=True)
    v = jnp.var(x, axis=axis, keepdims=True)
    return (x - m) / jnp.sqrt(v + eps)

def _scatter_add(tgt, idx, src, axis=0):
    return tgt.at[idx].add(src)

def _segment_sum(src, seg, n):
    return jax.ops.segment_sum(src, seg, n)
kernel_name = 'mk_metaformer_d1_conv_nchw128_r4_97de3a'

def setup_inputs(seed: int=0):
    np.random.seed(seed)
    _w = jnp.asarray

    def _rec_inputs():
        import jax
        import jax.numpy as jnp
        _gk = jax.random.key(seed)
        x = -0.0002928 + 1 * jax.random.normal(jax.random.fold_in(_gk, 1), (8, 32, 16, 16), jnp.float32)
        return x
    x = _rec_inputs()

    def _L0_conv_setup():
        import jax, jax.numpy as jnp
        import numpy as np
        B, C, H, W = (8, 32, 16, 16)

        def _conv1x1(t, w, b):
            return jnp.einsum('bchw,oc->bohw', t, w) + b[None, :, None, None]
        key = jax.random.key(seed)
        ks = jax.random.split(key, 6)
        s = 1.0 / np.sqrt(C)
        return {'x': jax.random.normal(ks[0], (B, C, H, W), dtype=jnp.float32), 'freq_weights': jnp.ones((C,), dtype=jnp.float32), 'wq': jax.random.normal(ks[1], (C, C), dtype=jnp.float32) * s, 'bq': jnp.zeros((C,), dtype=jnp.float32), 'wk': jax.random.normal(ks[2], (C, C), dtype=jnp.float32) * s, 'bk': jnp.zeros((C,), dtype=jnp.float32), 'wv': jax.random.normal(ks[3], (C, C), dtype=jnp.float32) * s, 'bv': jnp.zeros((C,), dtype=jnp.float32), 'wo': jax.random.normal(ks[4], (C, C), dtype=jnp.float32) * s, 'bo': jnp.zeros((C,), dtype=jnp.float32)}
    _L0_conv_all = _L0_conv_setup()
    _L0_conv_in = {k: v for k, v in _L0_conv_all.items() if k in ('freq_weights', 'wq', 'bq', 'wk', 'bk', 'wv', 'bv', 'wo', 'bo')}
    del _L0_conv_all

    def _L0_ffn_setup():
        import jax, jax.numpy as jnp
        import numpy as np
        B, S, D, E, H, O, K = (128, 512, 32, 16, 128, 32, 8)
        key = jax.random.key(seed)
        k0, k1, k2, k3 = jax.random.split(key, 4)
        x = jax.random.normal(k0, (B, S, D), dtype=jnp.float32)
        gate_w = jax.random.normal(k1, (E, D), dtype=jnp.float32) * (1.0 / np.sqrt(D))
        gate_b = jnp.zeros((E,), dtype=jnp.float32)
        weight1 = jax.random.uniform(k2, (E, D + 1, H), dtype=jnp.float32, minval=-1.0, maxval=1.0) * (1.0 / np.sqrt(D + 1))
        weight2 = jax.random.uniform(k3, (E, H + 1, O), dtype=jnp.float32, minval=-1.0, maxval=1.0) * (1.0 / np.sqrt(H + 1))
        return {'x': x, 'gate_w': gate_w, 'gate_b': gate_b, 'weight1': weight1, 'weight2': weight2}
    _L0_ffn_all = _L0_ffn_setup()
    _L0_ffn_in = {k: v for k, v in _L0_ffn_all.items() if k in ('gate_w', 'gate_b', 'weight1', 'weight2')}
    del _L0_ffn_all
    return {'x': x, 'L0_conv_freq_weights': _L0_conv_in['freq_weights'], 'L0_conv_wq': _L0_conv_in['wq'], 'L0_conv_bq': _L0_conv_in['bq'], 'L0_conv_wk': _L0_conv_in['wk'], 'L0_conv_bk': _L0_conv_in['bk'], 'L0_conv_wv': _L0_conv_in['wv'], 'L0_conv_bv': _L0_conv_in['bv'], 'L0_conv_wo': _L0_conv_in['wo'], 'L0_conv_bo': _L0_conv_in['bo'], 'L0_ffn_gate_w': _L0_ffn_in['gate_w'], 'L0_ffn_gate_b': _L0_ffn_in['gate_b'], 'L0_ffn_weight1': _L0_ffn_in['weight1'], 'L0_ffn_weight2': _L0_ffn_in['weight2']}

def reference(x, L0_conv_freq_weights, L0_conv_wq, L0_conv_bq, L0_conv_wk, L0_conv_bk, L0_conv_wv, L0_conv_bv, L0_conv_wo, L0_conv_bo, L0_ffn_gate_w, L0_ffn_gate_b, L0_ffn_weight1, L0_ffn_weight2):
    import jax
    import jax.numpy as jnp

    def _L0_conv_ref(x, freq_weights, wq, bq, wk, bk, wv, bv, wo, bo):
        import jax, jax.numpy as jnp
        import numpy as np
        B, C, H, W = (8, 32, 16, 16)

        def _conv1x1(t, w, b):
            return jnp.einsum('bchw,oc->bohw', t, w) + b[None, :, None, None]
        b, c, h, w = x.shape
        n = h * w
        fd = jnp.fft.fft2(x, axes=(-2, -1))
        mag = jnp.abs(fd)
        freq_attn = mag * freq_weights[None, :, None, None]
        refined_freq = freq_attn * jnp.exp(1j * jnp.angle(fd))
        refined = jnp.fft.ifft2(refined_freq, axes=(-2, -1)).real.astype(x.dtype)
        q = _conv1x1(refined, wq, bq).reshape(b, c, n)
        k = _conv1x1(refined, wk, bk).reshape(b, c, n)
        v = _conv1x1(refined, wv, bv).reshape(b, c, n)
        scores = jnp.einsum('bcn,bcm->bnm', q, k) / jnp.sqrt(jnp.asarray(c, x.dtype))
        attn = jax.nn.softmax(scores, axis=-1)
        out = jnp.einsum('bnm,bcm->bcn', attn, v).reshape(b, c, h, w)
        return _conv1x1(out, wo, bo)

    def _L0_ffn_ref(x, gate_w, gate_b, weight1, weight2):
        import jax, jax.numpy as jnp
        import numpy as np
        B, S, D, E, H, O, K = (128, 512, 32, 16, 128, 32, 8)
        Bn, Sn, Dn = x.shape
        logits = jnp.einsum('bsd,ed->bse', x, gate_w) + gate_b
        probs = jax.nn.softmax(logits, axis=1)
        vals, idx = jax.lax.top_k(probs.transpose(0, 2, 1), K)
        topv = vals.transpose(0, 2, 1)
        topi = idx.transpose(0, 2, 1)
        flat_idx = topi.reshape(Bn, K * E)
        gathered = jnp.take_along_axis(x, flat_idx[:, :, None], axis=1)
        gathered = gathered.reshape(Bn, K, E, Dn)
        pooled = jnp.einsum('bked,bke->bed', gathered, topv)
        ones = jnp.ones((E, Bn, 1), dtype=x.dtype)
        h = jnp.concatenate([pooled.transpose(1, 0, 2), ones], axis=-1)
        h = jax.nn.gelu(jnp.einsum('ebd,edh->ebh', h, weight1), approximate=False)
        h = jnp.concatenate([h, ones], axis=-1)
        out = jnp.einsum('ebh,eho->ebo', h, weight2)
        out = out.transpose(1, 0, 2)
        weighted = jnp.einsum('beo,bke->bkeo', out, topv).reshape(Bn, K * E, O)
        outputs = jnp.zeros((Bn, Sn, O), dtype=x.dtype)
        outputs = outputs.at[jnp.arange(Bn)[:, None], flat_idx].add(weighted)
        return outputs

    def _gn(v, G=32, eps=1e-05):
        B_, C_, H_, W_ = v.shape
        g = v.reshape(B_, G, C_ // G, H_, W_)
        m = jnp.mean(g, axis=(2, 3, 4), keepdims=True)
        s = jnp.var(g, axis=(2, 3, 4), keepdims=True)
        return ((g - m) / jnp.sqrt(s + eps)).reshape(v.shape)

    def _ln_c(v, eps=1e-06):
        m = jnp.mean(v, axis=1, keepdims=True)
        s = jnp.var(v, axis=1, keepdims=True)
        return (v - m) / jnp.sqrt(s + eps)

    def _ln_t(v, eps=1e-05):
        m = jnp.mean(v, axis=-1, keepdims=True)
        s = jnp.var(v, axis=-1, keepdims=True)
        return (v - m) / jnp.sqrt(s + eps)

    def _to_tokens(v):
        B_, C_, H_, W_ = v.shape
        return v.reshape(B_, C_, H_ * W_).transpose(0, 2, 1)

    def _from_tokens(t, like):
        B_, C_, H_, W_ = like.shape
        return t.transpose(0, 2, 1).reshape(B_, C_, H_, W_)
    x = x + _L0_conv_ref(_ln_c(x), L0_conv_freq_weights, L0_conv_wq, L0_conv_bq, L0_conv_wk, L0_conv_bk, L0_conv_wv, L0_conv_bv, L0_conv_wo, L0_conv_bo)
    t = _to_tokens(x)
    t = t + _L0_ffn_ref(_ln_t(t), L0_ffn_gate_w, L0_ffn_gate_b, L0_ffn_weight1, L0_ffn_weight2)
    x = _from_tokens(t, x)
    return x

_drawn_inputs = setup_inputs


def setup_inputs(seed=0):
    import zlib

    import numpy as np

    out = dict(_drawn_inputs(seed))
    spreads = {'L0_conv_freq_weights': (1.0, 0.2),
     'L0_conv_bq': (0.0, 0.1),
     'L0_conv_bk': (0.0, 0.8),
     'L0_conv_bv': (0.0, 0.1),
     'L0_conv_bo': (0.0, 0.1),
     'L0_ffn_gate_b': (0.0, 0.1)}
    factors = {'L0_ffn_gate_w': 8.0, 'L0_ffn_weight1': 8.0, 'L0_ffn_weight2': 8.0}
    for name, (base, spread) in spreads.items():
        noise = np.random.default_rng([zlib.crc32(name.encode()), seed]).standard_normal(out[name].shape)
        drawn = base * np.exp(spread * noise) if base else spread * noise
        out[name] = jnp.asarray(drawn.astype(out[name].dtype))
    for name, factor in factors.items():
        out[name] = (out[name] * factor).astype(out[name].dtype)
    return out
```

```python
from contextlib import ExitStack

import numpy as np

import concourse.bass as bass
from concourse import mybir

B, C, H, W = 8, 32, 16, 16
N = H * W
GROUPS = 2
B4 = B // GROUPS
P = B4 * C
HALF = N // 2
E, K, HID = 16, 8, 128
E4 = P // C
J = E // E4
LN_C_EPS, LN_T_EPS = 1e-6, 1e-5
SCALE = float(C) ** -0.5
NOT_A_LOGIT = float(np.finfo(np.float32).min)

F32 = mybir.dt.float32
ALU = mybir.AluOpType
ACT = mybir.ActivationFunctionType
AX = mybir.AxisListType

NORM_COLS = {"center": P, "average": P, "freq": 1, "bq": 1, "bk": 1, "bv": 1, "bo": 1}
PROJ_COLS = {"wq": P, "wk": P, "wv": P, "wo": P, "ident": P}
GATE_COLS = {"gate": GROUPS * P, "gate_b": P, "own_batch": P, "stack": P, "own_slot": P, "own_rows": GROUPS * P}
FFN_COLS = {"w1": J * HID, "w2": E * C, "b1": HID, "expert_of": P, "b2": E, "tiled_ident": GROUPS * P}


def columns(cols):
    at, out = 0, {}
    for name, width in cols.items():
        out[name] = slice(at, at + width)
        at += width
    return out, at


def build(nc, x, norm_pack, proj_pack, gate_pack, ffn_pack, out):
    with ExitStack() as ctx:
        def sb(name, shape):
            return ctx.enter_context(nc.sbuf_tensor(name, shape, F32))

        def sem(name):
            return ctx.enter_context(nc.semaphore(name))

        def unpack(name, cols):
            where, width = columns(cols)
            tile = sb(name, [P, width])
            return tile, {k: tile[:, s] for k, s in where.items()}

        norm_tile, nw = unpack("norm_tile", NORM_COLS)
        proj_tile, pw = unpack("proj_tile", PROJ_COLS)
        gate_tile, gw = unpack("gate_tile", GATE_COLS)
        ffn_tile, fw = unpack("ffn_tile", FFN_COLS)
        ident = pw["ident"]

        x_sb = sb("x_sb", [P, GROUPS, N])
        eps = sb("eps", [P, 2])
        sq = sb("sq", [P, GROUPS, N])
        log_var = sb("log_var", [P, GROUPS, N])
        rstd = sb("rstd", [P, GROUPS, N])
        y = sb("y", [P, GROUPS, N])
        q = sb("q", [P, GROUPS, N])
        k = sb("k", [P, GROUPS, N])
        wvo = sb("wvo", [P, P])
        bv_wide = sb("bv_wide", [P, HALF])
        v = sb("v", [P, GROUPS, 2, P])
        neg_max = sb("neg_max", [P, B, 2])
        row_sum = sb("row_sum", [P, B, 2])
        row_rcp = sb("row_rcp", [P, B, 2])
        expd = sb("expd", [P, 3, 2, N])
        probs = sb("probs", [P, 3, 2, N])
        probsT = sb("probsT", [P, 2, 2, N])
        t = sb("t", [P, GROUPS, N])
        tn = sb("tn", [P, GROUPS, N])
        tn_tok = sb("tn_tok", [P, GROUPS, 2, P])
        ones_row = sb("ones_row", [1, N])
        top = sb("top", [P, K])
        neg_top = sb("neg_top", [P, 1])
        marked = sb("marked", [P, N])
        chosen = sb("chosen", [P, N])
        gexp = sb("gexp", [P, N])
        gsum = sb("gsum", [P, 1])
        grcp = sb("grcp", [P, 1])
        gprob = sb("gprob", [P, N])
        gprobT = sb("gprobT", [P, 2, P])
        pooled = sb("pooled", [P, P])
        pooled_bd = sb("pooled_bd", [P, J, B, E4])
        hidden = sb("hidden", [P, J, B, E4])
        ffn_out = sb("ffn_out", [C, B, E])
        ffn_bd = sb("ffn_bd", [P, GROUPS * P])
        result = sb("result", [P, GROUPS, N])

        bank = [ctx.enter_context(nc.psum_tensor(f"bank{i}", [P, 512], F32)) for i in range(8)]
        xc_ps = [bank[6][:, 0:N], bank[7][:, 0:N]]
        var_ps = [bank[4][:, 0:N], bank[5][:, 0:N]]
        q_ps = [bank[6][:, 0:N], bank[7][:, 0:N]]
        k_ps = [bank[4][:, 0:N], bank[5][:, 0:N]]
        wvo_ps = bank[3][:, 0:P]
        v_ps = [bank[2][:, 0:2 * P], bank[3][:, 0:2 * P]]
        score_ps = [bank[i][:, :].rearrange("p (h m) -> p h m", h=2) for i in range(B4)]
        turn_ps = [bank[4 + i][:, :].rearrange("p (h n) -> p h n", h=2) for i in range(2)]
        attn_ps = [bank[6][:, 0:N], bank[7][:, 0:N]]
        xc2_ps = [bank[0][:, 0:N], bank[1][:, 0:N]]
        var2_ps = [bank[2][:, 0:N], bank[3][:, 0:N]]
        logit_ps = bank[4][:, 0:N]
        tok_ps = bank[0][:, :].rearrange("p (g h c) -> p g h c", g=GROUPS, h=2)
        gpT_ps = bank[5][:, 0:2 * P].rearrange("p (h r) -> p h r", h=2)
        pool_ps = bank[2][:, 0:P]
        stack_ps = bank[3][:, 0:P].rearrange("p (b j e) -> p j b e", b=B, j=J)
        hid_ps = bank[4][:, 0:P]
        eo_ps = bank[5][0:C, 0:P]
        tiled_ps = bank[6][:, 0:GROUPS * P]
        scat_ps = [bank[0][:, 0:N], bank[1][:, 0:N]]

        x_in = [sem(f"x_in{g}") for g in range(GROUPS)]
        norm_in, proj_in, gate_in, ffn_in = sem("norm_in"), sem("proj_in"), sem("gate_in"), sem("ffn_in")
        ready = sem("ready")
        xc_done, sq_done, var_done = sem("xc_done"), sem("sq_done"), sem("var_done")
        log_done, rstd_done, y_done = sem("log_done"), sem("rstd_done"), sem("y_done")
        wvo_done, wvo_copied = sem("wvo_done"), sem("wvo_copied")
        qp_done, kp_done, vp_done = sem("qp_done"), sem("kp_done"), sem("vp_done")
        q_done, k_done, v_done = sem("q_done"), sem("k_done"), sem("v_done")
        score_done, max_done, exp_done = sem("score_done"), sem("max_done"), sem("exp_done")
        rcp_done, probs_done = sem("rcp_done"), sem("probs_done")
        turn_done, turned, attn_done = sem("turn_done"), sem("turned"), sem("attn_done")
        t_done, xc2_done, sq2_done, var2_done = sem("t_done"), sem("xc2_done"), sem("sq2_done"), sem("var2_done")
        log2_done, rstd2_done, tn_done = sem("log2_done"), sem("rstd2_done"), sem("tn_done")
        logit_done, top_done, neg_done = sem("logit_done"), sem("top_done"), sem("neg_done")
        mark_done, chosen_done, gexp_done = sem("mark_done"), sem("chosen_done"), sem("gexp_done")
        grcp_done, gprob_done = sem("grcp_done"), sem("gprob_done")
        tok_done, tok_copied, gpT_done, gpT_copied = sem("tok_done"), sem("tok_copied"), sem("gpT_done"), sem("gpT_copied")
        pool_done, pool_copied, stack_done, stack_copied = sem("pool_done"), sem("pool_copied"), sem("stack_done"), sem("stack_copied")
        hid_done, gelu_done, eo_done, eo_copied = sem("hid_done"), sem("gelu_done"), sem("eo_done"), sem("eo_copied")
        tiled_done, tiled_copied, scat_done = sem("tiled_done"), sem("tiled_copied"), sem("scat_done")
        result_done, stored = sem("result_done"), sem("stored")

        x_cm = x.rearrange("(g b) c h w -> g (b c) (h w)", g=GROUPS)
        out_cm = out.rearrange("(g b) c h w -> g (b c) (h w)", g=GROUPS)

        block = ctx.enter_context(nc.Block())

        @block.sync
        def _(sp):
            sp.dma_start(x_sb[:, 0, :], x_cm[0]).then_inc(x_in[0], 16)
            sp.dma_start(x_sb[:, 1, :], x_cm[1]).then_inc(x_in[1], 16)
            sp.dma_start(gate_tile[:, :], gate_pack).then_inc(gate_in, 16)
            sp.wait_ge(result_done, 1)
            sp.dma_start(out_cm[0], result[:, 0, :]).then_inc(stored, 16)
            sp.wait_ge(result_done, 2)
            sp.dma_start(out_cm[1], result[:, 1, :]).then_inc(stored, 16)
            sp.wait_ge(stored, 16 * GROUPS)

        @block.scalar
        def _(act):
            act.dma_start(norm_tile[:, :], norm_pack).then_inc(norm_in, 16)
            act.dma_start(proj_tile[:, :], proj_pack).then_inc(proj_in, 16)
            act.dma_start(ffn_tile[:, :], ffn_pack).then_inc(ffn_in, 16)
            nc.scalar.preload_act_table_set("natural_log_exp_and_others")

            act.wait_ge(ready, 1)
            for g in range(GROUPS):
                act.wait_ge(xc_done, g + 1)
                nc.scalar.activation(sq[:, g, :], xc_ps[g], ACT.Square).then_inc(sq_done, 1)
            for g in range(GROUPS):
                act.wait_ge(var_done, g + 1)
                nc.scalar.activation(log_var[:, g, :], var_ps[g], ACT.Ln, bias=eps[:, 0:1]).then_inc(log_done, 1)
                act.wait_ge(log_done, g + 1)
                nc.scalar.activation(rstd[:, g, :], log_var[:, g, :], ACT.Exp, scale=-0.5).then_inc(rstd_done, 1)
            for g in range(GROUPS):
                act.wait_ge(kp_done, g + 1)
                nc.scalar.activation(k[:, g, :], k_ps[g], ACT.Identity, bias=nw["bk"]).then_inc(k_done, 1)

            def exponentials(b):
                act.wait_ge(max_done, b + 1)
                if b >= 3:
                    act.wait_ge(probs_done, b - 2)
                for h in range(2):
                    nc.scalar.activation(expd[:, b % 3, h, :], score_ps[b % B4][:, h, :], ACT.Exp,
                                         bias=neg_max[:, b, h:h + 1],
                                         accum_out=row_sum[:, b, h:h + 1]).then_inc(exp_done, 1)

            def evacuate_turned(b):
                act.wait_ge(turn_done, b + 1)
                if b >= 2:
                    act.wait_ge(attn_done, b - 1)
                nc.scalar.copy(probsT[:, b % 2, :, :], turn_ps[b % 2]).then_inc(turned, 1)

            for b in range(B + 1):
                if b < B:
                    exponentials(b)
                if b >= 1:
                    evacuate_turned(b - 1)

            for g in range(GROUPS):
                act.wait_ge(xc2_done, g + 1)
                nc.scalar.activation(sq[:, g, :], xc2_ps[g], ACT.Square).then_inc(sq2_done, 1)
                act.wait_ge(var2_done, g + 1)
                nc.scalar.activation(log_var[:, g, :], var2_ps[g], ACT.Ln, bias=eps[:, 1:2]).then_inc(log2_done, 1)
                act.wait_ge(log2_done, g + 1)
                nc.scalar.activation(rstd[:, g, :], log_var[:, g, :], ACT.Exp, scale=-0.5).then_inc(rstd2_done, 1)

            act.wait_ge(neg_done, 1)
            nc.scalar.activation(gexp[:, :], logit_ps, ACT.Exp, bias=neg_top[:, :],
                                 accum_out=gsum[:, :]).then_inc(gexp_done, 1)
            nc.scalar.preload_act_table(ACT.Gelu)
            act.wait_ge(tok_done, 1)
            nc.scalar.copy(tn_tok[:, :, :, :], tok_ps).then_inc(tok_copied, 1)
            act.wait_ge(hid_done, 1)
            nc.scalar.activation(hidden[:, :, :, :].rearrange("p j b e -> p (j b e)"), hid_ps,
                                 ACT.Gelu).then_inc(gelu_done, 1)

        @block.vector
        def _(dve):
            nc.vector.memset(eps[:, 0:1], LN_C_EPS)
            nc.vector.memset(eps[:, 1:2], LN_T_EPS).then_inc(ready, 1)
            nc.vector.memset(ones_row[:, :], 1.0).then_inc(ready, 1)
            nc.vector.memset(bv_wide[:, :], 0.0).then_inc(ready, 1)
            dve.wait_ge(norm_in, 16)
            dve.wait_ge(ready, 3)
            nc.vector.tensor_scalar(bv_wide[:, :], bv_wide[:, :], nw["bv"], None, ALU.add).then_inc(ready, 1)
            dve.wait_ge(wvo_done, 1)
            nc.vector.tensor_copy(wvo[:, :], wvo_ps).then_inc(wvo_copied, 1)
            for g in range(GROUPS):
                dve.wait_ge(rstd_done, g + 1)
                nc.vector.scalar_tensor_tensor(y[:, g, :], xc_ps[g], nw["freq"], rstd[:, g, :],
                                               ALU.mult, ALU.mult).then_inc(y_done, 1)
            for g in range(GROUPS):
                dve.wait_ge(qp_done, g + 1)
                nc.vector.tensor_scalar(q[:, g, :], q_ps[g], nw["bq"], SCALE, ALU.add,
                                        ALU.mult).then_inc(q_done, 1)
                dve.wait_ge(vp_done, g + 1)
                nc.vector.tensor_copy(v[:, g, :, :].rearrange("p h c -> p (h c)"), v_ps[g]).then_inc(v_done, 1)

            def row_maxima(b):
                dve.wait_ge(score_done, b + 1)
                nc.vector.tensor_reduce(neg_max[:, b, :], score_ps[b % B4], AX.X, ALU.max,
                                        negate=True).then_inc(max_done, 1)

            def normalise(b):
                dve.wait_ge(exp_done, 2 * (b + 1))
                nc.vector.reciprocal(row_rcp[:, b, :], row_sum[:, b, :]).then_inc(rcp_done, 1)
                dve.wait_ge(rcp_done, b + 1)
                if b >= 3:
                    dve.wait_ge(turn_done, b - 2)
                nc.vector.tensor_scalar(probs[:, b % 3, 0, :], expd[:, b % 3, 0, :],
                                        row_rcp[:, b, 0:1], None, ALU.mult)
                nc.vector.tensor_scalar(probs[:, b % 3, 1, :], expd[:, b % 3, 1, :],
                                        row_rcp[:, b, 1:2], None, ALU.mult).then_inc(probs_done, 1)

            def add_residual(g):
                dve.wait_ge(attn_done, B4 * (g + 1))
                nc.vector.scalar_tensor_tensor(t[:, g, :], attn_ps[g], nw["bo"], x_sb[:, g, :],
                                               ALU.add, ALU.add).then_inc(t_done, 1)

            row_maxima(0)
            for b in range(B):
                if b + 1 < B:
                    row_maxima(b + 1)
                normalise(b)
            add_residual(0)
            dve.wait_ge(rstd2_done, 1)
            nc.vector.tensor_tensor(tn[:, 0, :], xc2_ps[0], rstd[:, 0, :], ALU.mult).then_inc(tn_done, 1)
            add_residual(1)
            dve.wait_ge(rstd2_done, 2)
            nc.vector.tensor_tensor(tn[:, 1, :], xc2_ps[1], rstd[:, 1, :], ALU.mult).then_inc(tn_done, 1)

            dve.wait_ge(logit_done, 1)
            nc.vector.max(top[:, :], logit_ps).then_inc(top_done, 1)
            dve.wait_ge(top_done, 1)
            nc.vector.tensor_scalar(neg_top[:, :], top[:, 0:1], -1.0, None, ALU.mult).then_inc(neg_done, 1)
            dve.wait_ge(gexp_done, 1)
            nc.vector.match_replace(marked[:, :], top[:, :], logit_ps, NOT_A_LOGIT).then_inc(mark_done, 1)
            nc.vector.reciprocal(grcp[:, :], gsum[:, :]).then_inc(grcp_done, 1)
            dve.wait_ge(mark_done, 1)
            nc.vector.tensor_scalar(chosen[:, :], marked[:, :], NOT_A_LOGIT, None,
                                    ALU.is_equal).then_inc(chosen_done, 1)
            dve.wait_ge(chosen_done, 1)
            dve.wait_ge(grcp_done, 1)
            nc.vector.scalar_tensor_tensor(gprob[:, :], gexp[:, :], grcp[:, :], chosen[:, :],
                                           ALU.mult, ALU.mult).then_inc(gprob_done, 1)
            dve.wait_ge(gpT_done, 1)
            nc.vector.tensor_copy(gprobT[:, :, :], gpT_ps).then_inc(gpT_copied, 1)
            dve.wait_ge(pool_done, 1)
            nc.vector.tensor_tensor(pooled[:, :], pool_ps, gw["own_batch"], ALU.mult).then_inc(pool_copied, 1)
            dve.wait_ge(stack_done, 1)
            nc.vector.tensor_tensor(pooled_bd[:, :, :, :], stack_ps,
                                    gw["own_slot"].rearrange("p (j b e) -> p j b e", j=J, b=B),
                                    ALU.mult).then_inc(stack_copied, 1)
            dve.wait_ge(eo_done, 1)
            nc.vector.tensor_tensor(ffn_out[:, :, :], eo_ps.rearrange("o (e b) -> o b e", b=B),
                                    fw["b2"][0:C, :].unsqueeze(1).to_broadcast([C, B, E]),
                                    ALU.add).then_inc(eo_copied, 1)
            dve.wait_ge(tiled_done, 1)
            nc.vector.tensor_tensor(ffn_bd[:, :], tiled_ps, gw["own_rows"], ALU.mult).then_inc(tiled_copied, 1)
            for g in range(GROUPS):
                dve.wait_ge(scat_done, g + 1)
                nc.vector.tensor_tensor(result[:, g, :], scat_ps[g], t[:, g, :], ALU.add).then_inc(result_done, 1)

        @block.tensor
        def _(pe):
            mm = nc.tensor.matmul
            pe.wait_ge(norm_in, 16)
            for g in range(GROUPS):
                pe.wait_ge(x_in[g], 16)
                mm(xc_ps[g], nw["center"], x_sb[:, g, :], start=True, stop=True).then_inc(xc_done, 1)
            pe.wait_ge(proj_in, 16)
            mm(wvo_ps, pw["wv"], pw["wo"], start=True, stop=True).then_inc(wvo_done, 1)
            for g in range(GROUPS):
                pe.wait_ge(sq_done, g + 1)
                mm(var_ps[g], nw["average"], sq[:, g, :], start=True, stop=True).then_inc(var_done, 1)
            pe.wait_ge(ready, 4)
            pe.wait_ge(wvo_copied, 1)
            for g in range(GROUPS):
                pe.wait_ge(y_done, g + 1)
                mm(q_ps[g], pw["wq"], y[:, g, :], start=True, stop=True).then_inc(qp_done, 1)
                mm(k_ps[g], pw["wk"], y[:, g, :], start=True, stop=True).then_inc(kp_done, 1)
                for h in range(2):
                    vh = v_ps[g][:, h * P:(h + 1) * P]
                    mm(vh, y[:, g, h * HALF:(h + 1) * HALF], wvo[:, :], start=True, stop=False)
                    last = mm(vh, bv_wide[:, :], pw["wo"], start=False, stop=True)
                last.then_inc(vp_done, 1)

            def scores(pair):
                g = 2 * pair // B4
                pe.wait_ge(q_done, g + 1)
                pe.wait_ge(k_done, g + 1)
                if pair == 1:
                    pe.wait_ge(v_done, 2)
                for h in range(2):
                    for b in (2 * pair, 2 * pair + 1):
                        b4 = b % B4
                        if g and h == 0:
                            pe.wait_ge(exp_done, 2 * (b4 + 1))
                        rows = slice(C * b4, C * (b4 + 1))
                        s = mm(score_ps[b4][:, h, :], q[rows, g, h * HALF:(h + 1) * HALF], k[rows, g, :],
                               start=True, stop=True)
                        if h == 1:
                            s.then_inc(score_done, 1)

            def turn(b):
                pe.wait_ge(probs_done, b + 1)
                if b >= 2:
                    pe.wait_ge(turned, b - 1)
                for h in range(2):
                    for m in range(2):
                        last = nc.tensor.transpose(turn_ps[b % 2][:, m, h * HALF:(h + 1) * HALF],
                                                   probs[:, b % 3, h, m * HALF:(m + 1) * HALF], ident)
                last.then_inc(turn_done, 1)

            def attend(b):
                g, b4 = b // B4, b % B4
                pe.wait_ge(turned, b + 1)
                cols = slice(C * b4, C * (b4 + 1))
                for m in range(2):
                    last = mm(attn_ps[g][cols, :], v[:, g, m, cols], probsT[:, b % 2, m, :],
                              start=(m == 0), stop=(m == 1))
                last.then_inc(attn_done, 1)

            def centre(g):
                pe.wait_ge(t_done, g + 1)
                mm(xc2_ps[g], nw["center"], t[:, g, :], start=True, stop=True).then_inc(xc2_done, 1)

            def variance(g):
                pe.wait_ge(sq2_done, g + 1)
                mm(var2_ps[g], nw["average"], sq[:, g, :], start=True, stop=True).then_inc(var2_done, 1)

            scores(0)
            scores(1)
            for b in range(B):
                turn(b)
                if b >= 1:
                    attend(b - 1)
                if b in (1, 3):
                    scores(b // 2 + 2)
            attend(B - 1)
            pe.wait_ge(exp_done, 2 * B)
            centre(0)
            variance(0)
            centre(1)
            variance(1)

            pe.wait_ge(gate_in, 16)
            mm(logit_ps, gw["gate_b"][0:1, :], ones_row[:, :], start=True, stop=False)
            for g in range(GROUPS):
                pe.wait_ge(tn_done, g + 1)
                last = mm(logit_ps, gw["gate"][:, g * P:(g + 1) * P], tn[:, g, :],
                          start=False, stop=(g == GROUPS - 1))
            last.then_inc(logit_done, 1)
            for g in range(GROUPS):
                for h in range(2):
                    last = nc.tensor.transpose(tok_ps[:, g, h, :], tn[:, g, h * HALF:(h + 1) * HALF], ident)
            last.then_inc(tok_done, 1)
            pe.wait_ge(gprob_done, 1)
            for h in range(2):
                last = nc.tensor.transpose(gpT_ps[:, h, :], gprob[:, h * HALF:(h + 1) * HALF], ident)
            last.then_inc(gpT_done, 1)
            pe.wait_ge(gpT_copied, 1)
            pe.wait_ge(tok_copied, 1)
            for g in range(GROUPS):
                rows = slice(g * B4 * E, (g + 1) * B4 * E)
                for h in range(2):
                    last = mm(pool_ps[:, rows], tn_tok[:, g, h, :], gprobT[:, h, rows],
                              start=(h == 0), stop=(h == 1))
            last.then_inc(pool_done, 1)
            pe.wait_ge(pool_copied, 1)
            mm(bank[3][:, 0:P], gw["stack"], pooled[:, :], start=True, stop=True).then_inc(stack_done, 1)
            pe.wait_ge(ffn_in, 16)
            mm(hid_ps, fw["b1"][0:E, :], fw["expert_of"][0:E, :], start=True, stop=False, skip_group_check=True)
            pe.wait_ge(stack_copied, 1)
            for j in range(J):
                last = mm(hid_ps[:, j * B * E4:(j + 1) * B * E4], fw["w1"][:, j * HID:(j + 1) * HID],
                          pooled_bd[:, j, :, :].rearrange("p b e -> p (b e)"),
                          start=False, stop=(j == J - 1), skip_group_check=True)
            last.then_inc(hid_done, 1)
            pe.wait_ge(gelu_done, 1)
            for e in range(E):
                last = mm(eo_ps[:, e * B:(e + 1) * B], fw["w2"][:, e * C:(e + 1) * C],
                          hidden[:, e // E4, :, e % E4], start=True, stop=True)
            last.then_inc(eo_done, 1)
            pe.wait_ge(eo_copied, 1)
            mm(tiled_ps, ffn_out[:, :, :].rearrange("o b e -> o (b e)"), fw["tiled_ident"][0:C, :],
               start=True, stop=True).then_inc(tiled_done, 1)
            pe.wait_ge(tiled_copied, 1)
            for g in range(GROUPS):
                mm(scat_ps[g], ffn_bd[:, g * P:(g + 1) * P], gprob[:, :],
                   start=True, stop=True).then_inc(scat_done, 1)


def block_diagonal(w):
    r, c = w.shape
    d = np.zeros((B4, r, B4, c), w.dtype)
    for b4 in range(B4):
        d[b4, :, b4, :] = w
    return d.reshape(B4 * r, B4 * c)


def packed(cols, parts):
    where, width = columns(cols)
    a = np.zeros((P, width), np.float32)
    for name, part in parts.items():
        a[0:part.shape[0], where[name]] = part
    return a


def kernel(x, L0_conv_freq_weights, L0_conv_wq, L0_conv_bq, L0_conv_wk, L0_conv_bk, L0_conv_wv, L0_conv_bv,
           L0_conv_wo, L0_conv_bo, L0_ffn_gate_w, L0_ffn_gate_b, L0_ffn_weight1, L0_ffn_weight2):
    import concourse.bacc as bacc
    from concourse.bass_utils import run_bass_kernel_spmd

    f = lambda a: np.asarray(a)
    eye = np.eye(C, dtype=np.float32)
    average = block_diagonal(np.full((C, C), 1.0 / C, np.float32))
    per_channel = lambda a: np.tile(f(a), B4).reshape(P, 1)
    row = np.arange(P)

    gate = np.zeros((P, GROUPS, GROUPS, B4 * E), np.float32)
    for g in range(GROUPS):
        gate[:, g, g, :] = block_diagonal(f(L0_ffn_gate_w).T)
    slot = np.zeros((E4, C, J, B, E4), np.float32)
    for e4 in range(E4):
        slot[e4, :, :, :, e4] = 1.0
    expert = np.zeros((J, E4, J, B, E4), np.float32)
    for e in range(E):
        expert[e // E4, e % E4, e // E4, :, e % E4] = 1.0
    w1, w2 = f(L0_ffn_weight1), f(L0_ffn_weight2)

    arrays = {
        "x": np.ascontiguousarray(f(x)),
        "norm_pack": packed(NORM_COLS, {
            "center": np.eye(P, dtype=np.float32) - average, "average": average,
            "freq": per_channel(L0_conv_freq_weights), "bq": per_channel(L0_conv_bq),
            "bk": per_channel(L0_conv_bk), "bv": per_channel(L0_conv_bv), "bo": per_channel(L0_conv_bo)}),
        "proj_pack": packed(PROJ_COLS, {
            "wq": block_diagonal(f(L0_conv_wq).T), "wk": block_diagonal(f(L0_conv_wk).T),
            "wv": block_diagonal(f(L0_conv_wv)), "wo": block_diagonal(f(L0_conv_wo).T),
            "ident": np.eye(P, dtype=np.float32)}),
        "gate_pack": packed(GATE_COLS, {
            "gate": gate.reshape(P, GROUPS * P), "gate_b": np.tile(f(L0_ffn_gate_b), B).reshape(1, P),
            "own_batch": (row[:, None] // C == (row[None, :] // E) % B4).astype(np.float32),
            "stack": np.tile(eye, (B4, B4)),
            "own_slot": slot.reshape(P, P),
            "own_rows": (row[:, None] // E == np.arange(GROUPS * P)[None, :] // C).astype(np.float32)}),
        "ffn_pack": packed(FFN_COLS, {
            "w1": w1[:, 0:C, :].reshape(J, E4, C, HID).transpose(1, 2, 0, 3).reshape(P, J * HID),
            "w2": w2[:, 0:HID, :].transpose(1, 0, 2).reshape(HID, E * C),
            "b1": w1[:, C, :], "expert_of": expert.reshape(E, P),
            "b2": w2[:, HID, :].T, "tiled_ident": np.tile(eye, (1, B))}),
    }
    nc = bacc.Bacc("TRN2", target_bir_lowering=False, num_devices=1)
    args = [nc.dram_tensor(n, a.shape, F32, kind="ExternalInput").ap() for n, a in arrays.items()]
    out = nc.dram_tensor("out", (B, C, H, W), F32, kind="ExternalOutput").ap()
    build(nc, *args, out)
    r = run_bass_kernel_spmd(nc, [arrays], core_ids=[0])
    return r.results[0]["out"]
```

```python
from contextlib import ExitStack

import numpy as np

import concourse.bass as bass
from concourse import mybir

B, C, H, W = 8, 32, 16, 16
N = H * W
GROUPS = 2
B4 = B // GROUPS
P = B4 * C
HALF = N // 2
E, K, HID = 16, 8, 128
E4 = P // C
J = E // E4
START_WARM = 6
TAIL_WARM = (1, 2, 1, 2, 5, 3, 2, 2, 2, 2, 2)
LN_C_EPS, LN_T_EPS = 1e-6, 1e-5
SCALE = float(C) ** -0.5
P_SCALE = 4096.0
PARTS = 3
NOT_A_LOGIT = float(np.finfo(np.float32).min)

F32 = mybir.dt.float32
BF16 = mybir.dt.bfloat16
F16 = mybir.dt.float16
ALU = mybir.AluOpType
ACT = mybir.ActivationFunctionType
AX = mybir.AxisListType

NORM_COLS = {"center": P, "average": P, "freq": 1, "bq": 1, "bk": 1, "bv": 1, "bo": 1}
PROJ_COLS = {"wq": P, "wk": P, "wv": P, "wo": P, "ident": P}
GATE_COLS = {"gate": GROUPS * P, "gate_b": P, "own_batch": P, "stack": P, "own_slot": P, "own_rows": GROUPS * P}
FFN_COLS = {"w1": J * HID, "w2": E * C, "b1": HID, "expert_of": P, "row_expert": P, "b2": C, "tiled_ident": GROUPS * P}


def columns(cols):
    at, out = 0, {}
    for name, width in cols.items():
        out[name] = slice(at, at + width)
        at += width
    return out, at


def build(nc, x, norm_pack, proj_pack, gate_pack, ffn_pack, out):
    with ExitStack() as ctx:
        def sb(name, shape, dtype=F32):
            return ctx.enter_context(nc.sbuf_tensor(name, shape, dtype))

        def sem(name):
            return ctx.enter_context(nc.semaphore(name))

        def unpack(name, cols):
            where, width = columns(cols)
            tile = sb(name, [P, width])
            return tile, {k: tile[:, s] for k, s in where.items()}

        norm_tile, nw = unpack("norm_tile", NORM_COLS)
        proj_tile, pw = unpack("proj_tile", PROJ_COLS)
        gate_tile, gw = unpack("gate_tile", GATE_COLS)
        ffn_tile, fw = unpack("ffn_tile", FFN_COLS)
        ident = pw["ident"]

        x_sb = sb("x_sb", [P, GROUPS, N])
        eps = sb("eps", [P, 2])
        sq = sb("sq", [P, GROUPS, N])
        log_var = sb("log_var", [P, GROUPS, N])
        rstd = sb("rstd", [P, GROUPS, N])
        y = sb("y", [P, GROUPS, N])
        q = sb("q", [P, GROUPS, N])
        k = sb("k", [P, GROUPS, N])
        wvo = sb("wvo", [P, P])
        bias_out = sb("bias_out", [P, 1])
        x_bias = sb("x_bias", [P, GROUPS, N])
        v = sb("v", [P, GROUPS, 2, B4, C])
        v_rest = sb("v_rest", [P, GROUPS, 2, B4, C])
        v_parts = sb("v_parts", [P, GROUPS, 2, B4, PARTS, C], BF16)
        neg_max = sb("neg_max", [P, B, 2])
        row_sum = sb("row_sum", [P, B, 2])
        row_rcp = sb("row_rcp", [P, B, 2])
        expd = sb("expd", [P, 3, 2, N])
        p_hi = sb("p_hi", [P, 2, 2, N], F16)
        p_lo = sb("p_lo", [P, 2, 2, N], F16)
        attn_sum = sb("attn_sum", [P, 2, 2, C])
        attn = sb("attn", [P, GROUPS, 2, B4, C])
        t = sb("t", [P, GROUPS, N])
        tn = sb("tn", [P, GROUPS, N])
        tn_tok = sb("tn_tok", [P, GROUPS, 2, P])
        ones_row = sb("ones_row", [1, N])
        top = sb("top", [P, K])
        neg_top = sb("neg_top", [P, 1])
        marked = sb("marked", [P, N])
        chosen = sb("chosen", [P, N])
        gexp = sb("gexp", [P, N])
        gsum = sb("gsum", [P, 1])
        grcp = sb("grcp", [P, 1])
        gprob = sb("gprob", [P, N])
        gprobT = sb("gprobT", [P, 2, P])
        pooled = sb("pooled", [P, P])
        pooled_bd = sb("pooled_bd", [P, J, B, E4])
        hidden = sb("hidden", [P, J, B, E4])
        ffn_out = sb("ffn_out", [P, B, J, E4])
        ffn_bd = sb("ffn_bd", [P, GROUPS * P])
        result = sb("result", [P, GROUPS, N])
        warm = sb("warm", [P, 1], BF16)

        bank = [ctx.enter_context(nc.psum_tensor(f"bank{i}", [P, 512], F32)) for i in range(8)]
        xc_ps = [bank[6][:, 0:N], bank[7][:, 0:N]]
        var_ps = [bank[4][:, 0:N], bank[5][:, 0:N]]
        q_ps = [bank[6][:, 0:N], bank[7][:, 0:N]]
        k_ps = [bank[4][:, 0:N], bank[5][:, 0:N]]
        wvo_ps = bank[3][:, 0:P]
        bias_ps = bank[3][:, P:P + 1]
        v_ps = [bank[2][:, 0:2 * P], bank[5][:, 0:2 * P]]
        score_ps = [bank[i][:, :].rearrange("p (h m) -> p h m", h=2) for i in range(B4)]
        turn_ps = [bank[4 + i][:, :].rearrange("p (h n) -> p h n", h=2) for i in range(2)]
        attn_ps = [bank[6 + i][:, 0:4 * PARTS * C].rearrange("p (b h s) -> p b h s", b=2, h=2) for i in range(2)]
        back_ps = [bank[0][:, 0:N], bank[2][:, 0:N]]
        xc2_ps = [bank[1][:, 0:N], bank[3][:, 0:N]]
        var2_ps = [bank[0][:, 0:N], bank[2][:, 0:N]]
        logit_ps = bank[4][:, 0:N]
        tok_ps = bank[0][:, :].rearrange("p (g h c) -> p g h c", g=GROUPS, h=2)
        gpT_ps = bank[5][:, 0:2 * P].rearrange("p (h r) -> p h r", h=2)
        pool_ps = bank[2][:, 0:P]
        stack_ps = bank[3][:, 0:P].rearrange("p (b j e) -> p j b e", b=B, j=J)
        hid_ps = bank[1][:, 0:P]
        eo_ps = bank[5][:, 0:P]
        tiled_ps = bank[6][:, 0:GROUPS * P]
        scat_ps = [bank[0][:, 0:N], bank[1][:, 0:N]]

        x_in = [sem(f"x_in{g}") for g in range(GROUPS)]
        norm_in, proj_in, gate_in, ffn_in = sem("norm_in"), sem("proj_in"), sem("gate_in"), sem("ffn_in")
        ready = sem("ready")
        xc_done, sq_done, var_done = sem("xc_done"), sem("sq_done"), sem("var_done")
        log_done, rstd_done, y_done = sem("log_done"), sem("rstd_done"), sem("y_done")
        wvo_done, wvo_copied = sem("wvo_done"), sem("wvo_copied")
        qp_done, kp_done, vp_done = sem("qp_done"), sem("kp_done"), sem("vp_done")
        q_done, k_done, v_done = sem("q_done"), sem("k_done"), sem("v_done")
        score_done, max_done, exp_done = sem("score_done"), sem("max_done"), sem("exp_done")
        rcp_done, bias_done = sem("rcp_done"), sem("bias_done")
        turn_done, hi_done, lo_done, attn_done = sem("turn_done"), sem("hi_done"), sem("lo_done"), sem("attn_done")
        split_step, split_done, x_bias_done = sem("split_step"), sem("split_done"), sem("x_bias_done")
        summed, scaled, back_done = sem("summed"), sem("scaled"), sem("back_done")
        t_done, xc2_done, sq2_done, var2_done = sem("t_done"), sem("xc2_done"), sem("sq2_done"), sem("var2_done")
        log2_done, rstd2_done, tn_done = sem("log2_done"), sem("rstd2_done"), sem("tn_done")
        logit_done, top_done, neg_done = sem("logit_done"), sem("top_done"), sem("neg_done")
        mark_done, chosen_done, gexp_done = sem("mark_done"), sem("chosen_done"), sem("gexp_done")
        grcp_done, gprob_done = sem("grcp_done"), sem("gprob_done")
        tok_done, tok_copied, gpT_done, gpT_copied = sem("tok_done"), sem("tok_copied"), sem("gpT_done"), sem("gpT_copied")
        pool_done, pool_copied, stack_done, stack_copied = sem("pool_done"), sem("pool_copied"), sem("stack_done"), sem("stack_copied")
        hid_done, gelu_done, eo_done, eo_copied = sem("hid_done"), sem("gelu_done"), sem("eo_done"), sem("eo_copied")
        tiled_done, tiled_copied, scat_done = sem("tiled_done"), sem("tiled_copied"), sem("scat_done")
        result_done, stored = sem("result_done"), sem("stored")

        x_cm = x.rearrange("(g b) c h w -> g (b c) (h w)", g=GROUPS)
        out_cm = out.rearrange("(g b) c h w -> g (b c) (h w)", g=GROUPS)

        block = ctx.enter_context(nc.Block())

        @block.sync
        def _(sp):
            sp.dma_start(x_sb[:, 0, :], x_cm[0]).then_inc(x_in[0], 16)
            sp.dma_start(x_sb[:, 1, :], x_cm[1]).then_inc(x_in[1], 16)
            sp.dma_start(proj_tile[:, :], proj_pack).then_inc(proj_in, 16)
            sp.dma_start(gate_tile[:, :], gate_pack).then_inc(gate_in, 16)
            sp.dma_start(ffn_tile[:, :], ffn_pack).then_inc(ffn_in, 16)
            sp.wait_ge(result_done, 1)
            sp.dma_start(out_cm[0], result[:, 0, :]).then_inc(stored, 16)
            sp.wait_ge(stored, 16 * GROUPS)

        @block.gpsimd
        def _(pool):
            def step(ins, n):
                ins.then_inc(split_step, 1)
                pool.wait_ge(split_step, n)

            pool.wait_ge(bias_done, 1)
            pool.wait_ge(x_in[0], 16)
            pool.wait_ge(x_in[1], 16)
            for g in range(GROUPS):
                pool.wait_ge(v_done, g + 1)
                part = [v_parts[:, g, :, :, s, :] for s in range(PARTS)]
                step(nc.gpsimd.tensor_tensor(v_rest[:, g], v[:, g], part[0], ALU.subtract), 2 * g + 1)
                step(nc.gpsimd.tensor_copy(part[1], v_rest[:, g]), 2 * g + 2)
                nc.gpsimd.tensor_tensor(part[2], v_rest[:, g], part[1], ALU.subtract).then_inc(split_done, 1)
            nc.gpsimd.tensor_scalar(x_bias[:, :, :], x_sb[:, :, :], bias_out[:, :], 1.0, ALU.add,
                                    ALU.mult).then_inc(x_bias_done, 1)

        @block.scalar
        def _(act):
            act.dma_start(norm_tile[:, :], norm_pack).then_inc(norm_in, 16)
            nc.scalar.preload_act_table_set("natural_log_exp_and_others")

            act.wait_ge(ready, 3)
            for g in range(GROUPS):
                act.wait_ge(xc_done, g + 1)
                nc.scalar.activation(sq[:, g, :], xc_ps[g], ACT.Square).then_inc(sq_done, 1)
            for g in range(GROUPS):
                act.wait_ge(var_done, g + 1)
                nc.scalar.activation(log_var[:, g, :], var_ps[g], ACT.Ln, bias=eps[:, 0:1]).then_inc(log_done, 1)
                act.wait_ge(log_done, g + 1)
                nc.scalar.activation(rstd[:, g, :], log_var[:, g, :], ACT.Exp, scale=-0.5).then_inc(rstd_done, 1)
            for g in range(GROUPS):
                act.wait_ge(kp_done, g + 1)
                nc.scalar.activation(k[:, g, :], k_ps[g], ACT.Identity, bias=nw["bk"]).then_inc(k_done, 1)

            for g in range(GROUPS):
                act.wait_ge(vp_done, g + 1)
                nc.scalar.copy(v_parts[:, g, :, :, 0, :], v_ps[g].rearrange("p (h b c) -> p h b c", h=2, b=B4))
                nc.scalar.copy(v[:, g].rearrange("p h b c -> p (h b c)"), v_ps[g]).then_inc(v_done, 1)

            def exponentials(b):
                act.wait_ge(max_done, b + 1)
                if b >= 3:
                    act.wait_ge(turn_done, b - 2)
                for h in range(2):
                    nc.scalar.activation(expd[:, b % 3, h, :], score_ps[b % B4][:, h, :], ACT.Exp,
                                         bias=neg_max[:, b, h:h + 1],
                                         accum_out=row_sum[:, b, h:h + 1]).then_inc(exp_done, 1)

            def high_part(b):
                act.wait_ge(turn_done, b + 1)
                if b >= 2:
                    act.wait_ge(attn_done, b - 1)
                nc.scalar.activation(p_hi[:, b % 2], turn_ps[b % 2], ACT.Identity,
                                     scale=P_SCALE).then_inc(hi_done, 1)

            def square(g):
                act.wait_ge(xc2_done, g + 1)
                nc.scalar.activation(sq[:, g, :], xc2_ps[g], ACT.Square).then_inc(sq2_done, 1)

            def inverse_deviation(g):
                act.wait_ge(var2_done, g + 1)
                nc.scalar.activation(log_var[:, g, :], var2_ps[g], ACT.Ln, bias=eps[:, 1:2]).then_inc(log2_done, 1)
                act.wait_ge(log2_done, g + 1)
                nc.scalar.activation(rstd[:, g, :], log_var[:, g, :], ACT.Exp, scale=-0.5).then_inc(rstd2_done, 1)

            for b in range(B + 1):
                if b < B:
                    exponentials(b)
                if b >= 1:
                    high_part(b - 1)
                if b == B - 1:
                    square(0)
            inverse_deviation(0)
            square(1)
            inverse_deviation(1)

            act.wait_ge(neg_done, 1)
            act.wait_ge(mark_done, 1)
            nc.scalar.activation(gexp[:, :], logit_ps, ACT.Exp, bias=neg_top[:, :],
                                 accum_out=gsum[:, :]).then_inc(gexp_done, 1)
            act.wait_ge(tok_done, 1)
            nc.scalar.copy(tn_tok[:, :, :, :], tok_ps).then_inc(tok_copied, 1)
            nc.scalar.preload_act_table(ACT.Gelu)
            act.wait_ge(hid_done, 1)
            nc.scalar.activation(hidden[:, :, :, :].rearrange("p j b e -> p (j b e)"), hid_ps,
                                 ACT.Gelu).then_inc(gelu_done, 1)
            act.wait_ge(result_done, 2)
            act.dma_start(out_cm[1], result[:, 1, :]).then_inc(stored, 16)

        @block.vector
        def _(dve):
            nc.vector.memset(warm[:, :], 0.0).then_inc(ready, 1)
            nc.vector.memset(eps[:, 0:1], LN_C_EPS).then_inc(ready, 1)
            nc.vector.memset(eps[:, 1:2], LN_T_EPS).then_inc(ready, 1)
            nc.vector.memset(ones_row[:, :], 1.0).then_inc(ready, 1)
            dve.wait_ge(wvo_done, 1)
            nc.vector.tensor_copy(wvo[:, :], wvo_ps).then_inc(wvo_copied, 1)
            dve.wait_ge(norm_in, 16)
            nc.vector.tensor_scalar(bias_out[:, :], bias_ps, nw["bo"], None, ALU.add).then_inc(bias_done, 1)
            for g in range(GROUPS):
                dve.wait_ge(rstd_done, g + 1)
                nc.vector.scalar_tensor_tensor(y[:, g, :], xc_ps[g], nw["freq"], rstd[:, g, :],
                                               ALU.mult, ALU.mult).then_inc(y_done, 1)
            for g in range(GROUPS):
                dve.wait_ge(qp_done, g + 1)
                nc.vector.tensor_scalar(q[:, g, :], q_ps[g], nw["bq"], SCALE, ALU.add,
                                        ALU.mult).then_inc(q_done, 1)

            def row_maxima(b):
                dve.wait_ge(score_done, b + 1)
                nc.vector.tensor_reduce(neg_max[:, b, :], score_ps[b % B4], AX.X, ALU.max,
                                        negate=True).then_inc(max_done, 1)

            def low_part(b):
                dve.wait_ge(hi_done, b + 1)
                nc.vector.scalar_tensor_tensor(p_lo[:, b % 2].rearrange("p m n -> p (m n)"),
                                               turn_ps[b % 2].rearrange("p m n -> p (m n)"), P_SCALE,
                                               p_hi[:, b % 2].rearrange("p m n -> p (m n)"),
                                               ALU.mult, ALU.subtract).then_inc(lo_done, 1)

            def combine(pair):
                g, bs = 2 * pair // B4, slice(2 * pair % B4, 2 * pair % B4 + 2)
                batches = slice(2 * pair, 2 * pair + 2)
                dve.wait_ge(exp_done, 4 * (pair + 1))
                nc.vector.reciprocal(row_rcp[:, batches, :], row_sum[:, batches, :]).then_inc(rcp_done, 1)
                dve.wait_ge(attn_done, 2 * (pair + 1))
                nc.vector.tensor_reduce(attn_sum[:, :, :, :].rearrange("p b h c -> p (b h) c"),
                                        attn_ps[pair % 2].rearrange("p b h (s c) -> p (b h) c s", s=PARTS),
                                        AX.X, ALU.add).then_inc(summed, 1)
                dve.wait_ge(summed, pair + 1)
                dve.wait_ge(rcp_done, pair + 1)
                nc.vector.tensor_tensor(attn[:, g, :, bs, :].rearrange("p h b c -> p b h c"), attn_sum[:, :, :, :],
                                        row_rcp[:, batches, :].unsqueeze(3).to_broadcast([P, 2, 2, C]),
                                        ALU.mult).then_inc(scaled, 1)

            def add_residual(g):
                dve.wait_ge(back_done, g + 1)
                dve.wait_ge(x_bias_done, 1)
                nc.vector.scalar_tensor_tensor(t[:, g, :], back_ps[g], 1.0 / P_SCALE, x_bias[:, g, :],
                                               ALU.mult, ALU.add).then_inc(t_done, 1)

            def normalise(g):
                dve.wait_ge(rstd2_done, g + 1)
                nc.vector.tensor_tensor(tn[:, g, :], xc2_ps[g], rstd[:, g, :], ALU.mult).then_inc(tn_done, 1)

            row_maxima(0)
            row_maxima(1)
            for b in range(B):
                if b + 2 < B:
                    row_maxima(b + 2)
                low_part(b)
                if b in (2, 4):
                    combine(b // 2 - 1)
                if b == 5:
                    add_residual(0)
                if b == 6:
                    combine(2)
            combine(3)
            add_residual(1)
            normalise(0)
            normalise(1)

            dve.wait_ge(logit_done, 1)
            nc.vector.max(top[:, :], logit_ps).then_inc(top_done, 1)
            dve.wait_ge(top_done, 1)
            nc.vector.tensor_scalar(neg_top[:, :], top[:, 0:1], -1.0, None, ALU.mult).then_inc(neg_done, 1)
            nc.vector.match_replace(marked[:, :], top[:, :], logit_ps, NOT_A_LOGIT).then_inc(mark_done, 1)
            dve.wait_ge(mark_done, 1)
            nc.vector.tensor_scalar(chosen[:, :], marked[:, :], NOT_A_LOGIT, None,
                                    ALU.is_equal).then_inc(chosen_done, 1)
            dve.wait_ge(gexp_done, 1)
            nc.vector.reciprocal(grcp[:, :], gsum[:, :]).then_inc(grcp_done, 1)
            dve.wait_ge(chosen_done, 1)
            dve.wait_ge(grcp_done, 1)
            nc.vector.scalar_tensor_tensor(gprob[:, :], gexp[:, :], grcp[:, :], chosen[:, :],
                                           ALU.mult, ALU.mult).then_inc(gprob_done, 1)
            dve.wait_ge(gpT_done, 1)
            nc.vector.tensor_copy(gprobT[:, :, :], gpT_ps).then_inc(gpT_copied, 1)
            dve.wait_ge(pool_done, 1)
            nc.vector.tensor_tensor(pooled[:, :], pool_ps, gw["own_batch"], ALU.mult).then_inc(pool_copied, 1)
            dve.wait_ge(stack_done, 1)
            nc.vector.tensor_tensor(pooled_bd[:, :, :, :], stack_ps,
                                    gw["own_slot"].rearrange("p (j b e) -> p j b e", j=J, b=B),
                                    ALU.mult).then_inc(stack_copied, 1)
            dve.wait_ge(eo_done, 1)
            nc.vector.tensor_tensor(ffn_out[:, :, :, :].rearrange("p b j e -> p j b e"),
                                    eo_ps.rearrange("p (j b e) -> p j b e", j=J, b=B),
                                    gw["own_slot"].rearrange("p (j b e) -> p j b e", j=J, b=B),
                                    ALU.mult).then_inc(eo_copied, 1)
            dve.wait_ge(tiled_done, 1)
            nc.vector.tensor_tensor(ffn_bd[:, :], tiled_ps, gw["own_rows"], ALU.mult).then_inc(tiled_copied, 1)
            for g in range(GROUPS):
                dve.wait_ge(scat_done, g + 1)
                nc.vector.tensor_tensor(result[:, g, :], scat_ps[g], t[:, g, :], ALU.add).then_inc(result_done, 1)

        @block.tensor
        def _(pe):
            mm = nc.tensor.matmul

            def keep_warm(n, spare=bank[7]):
                for _ in range(n):
                    mm(spare[:, :], warm[:, :].to_broadcast([P, P]), warm[:, :].to_broadcast([P, 512]),
                       start=True, stop=True)

            pe.wait_ge(ready, 1)
            keep_warm(START_WARM)
            pe.wait_ge(norm_in, 16)
            for g in range(GROUPS):
                pe.wait_ge(x_in[g], 16)
                mm(xc_ps[g], nw["center"], x_sb[:, g, :], start=True, stop=True).then_inc(xc_done, 1)
            for g in range(GROUPS):
                pe.wait_ge(sq_done, g + 1)
                mm(var_ps[g], nw["average"], sq[:, g, :], start=True, stop=True).then_inc(var_done, 1)
            pe.wait_ge(proj_in, 16)
            mm(bias_ps, pw["wo"], nw["bv"], start=True, stop=True)
            mm(wvo_ps, pw["wv"], pw["wo"], start=True, stop=True).then_inc(wvo_done, 1)
            keep_warm(1, bank[0])
            for g in range(GROUPS):
                pe.wait_ge(y_done, g + 1)
                mm(q_ps[g], pw["wq"], y[:, g, :], start=True, stop=True).then_inc(qp_done, 1)
                mm(k_ps[g], pw["wk"], y[:, g, :], start=True, stop=True).then_inc(kp_done, 1)

            def values(g):
                pe.wait_ge(wvo_copied, 1)
                if g == 1:
                    pe.wait_ge(k_done, 2)
                for h in range(2):
                    last = mm(v_ps[g][:, h * P:(h + 1) * P], y[:, g, h * HALF:(h + 1) * HALF], wvo[:, :],
                              start=True, stop=True)
                last.then_inc(vp_done, 1)

            def scores(pair):
                g = 2 * pair // B4
                pe.wait_ge(q_done, g + 1)
                pe.wait_ge(k_done, g + 1)
                if pair == 1:
                    pe.wait_ge(v_done, 1)
                    pe.wait_ge(bias_done, 1)
                for h in range(2):
                    for b in (2 * pair, 2 * pair + 1):
                        b4 = b % B4
                        if g and h == 0:
                            pe.wait_ge(exp_done, 2 * (b4 + 1))
                        rows = slice(C * b4, C * (b4 + 1))
                        s = mm(score_ps[b4][:, h, :], q[rows, g, h * HALF:(h + 1) * HALF], k[rows, g, :],
                               start=True, stop=True)
                        if h == 1:
                            s.then_inc(score_done, 1)

            def turn(b):
                pe.wait_ge(exp_done, 2 * (b + 1))
                if b == 1:
                    pe.wait_ge(v_done, 2)
                if b >= 2:
                    pe.wait_ge(lo_done, b - 1)
                for h in range(2):
                    for m in range(2):
                        last = nc.tensor.transpose(turn_ps[b % 2][:, m, h * HALF:(h + 1) * HALF],
                                                   expd[:, b % 3, h, m * HALF:(m + 1) * HALF], ident)
                last.then_inc(turn_done, 1)

            def attend(b):
                g, b4, pair = b // B4, b % B4, b // 2
                if b % B4 == 0:
                    pe.wait_ge(split_done, g + 1)
                if b % 2 == 0 and pair >= 2:
                    pe.wait_ge(summed, pair - 1)
                pe.wait_ge(lo_done, b + 1)
                for h in range(2):
                    terms = [(part, m) for m in range(2) for part in (p_hi, p_lo)]
                    for i, (part, m) in enumerate(terms):
                        last = mm(attn_ps[pair % 2][:, b % 2, h, :],
                                  part[:, b % 2, m, h * HALF:(h + 1) * HALF],
                                  v_parts[:, g, m, b4].rearrange("p s c -> p (s c)"),
                                  start=(i == 0), stop=(i == len(terms) - 1))
                last.then_inc(attn_done, 1)

            def turn_back(g):
                pe.wait_ge(scaled, 2 * (g + 1))
                pe.wait_ge(exp_done, 2 * B4 + 2 * (1 if g == 0 else 3))
                for h in range(2):
                    last = nc.tensor.transpose(back_ps[g][:, h * HALF:(h + 1) * HALF],
                                               attn[:, g, h].rearrange("p b c -> p (b c)"), ident)
                last.then_inc(back_done, 1)

            def centre(g):
                pe.wait_ge(t_done, g + 1)
                pe.wait_ge(exp_done, 2 * B4 + 2 * (2 if g == 0 else 4))
                mm(xc2_ps[g], nw["center"], t[:, g, :], start=True, stop=True).then_inc(xc2_done, 1)

            def variance(g):
                pe.wait_ge(sq2_done, g + 1)
                mm(var2_ps[g], nw["average"], sq[:, g, :], start=True, stop=True).then_inc(var2_done, 1)

            scores(0)
            values(0)
            values(1)
            scores(1)
            for b in range(B):
                turn(b)
                if b in (1, 3):
                    scores(b // 2 + 2)
                if b == 5:
                    turn_back(0)
                if b == 6:
                    centre(0)
                if b >= 1:
                    attend(b - 1)
            pe.wait_ge(exp_done, 2 * B)
            keep_warm(TAIL_WARM[0], bank[3])
            attend(B - 1)
            variance(0)
            pe.wait_ge(gate_in, 16)
            pe.wait_ge(ffn_in, 16)
            pe.wait_ge(ready, 4)
            pe.wait_ge(lo_done, B)
            pe.wait_ge(summed, B4 - 1)
            mm(logit_ps, gw["gate_b"][0:1, :], ones_row[:, :], start=True, stop=False)
            mm(tiled_ps, fw["row_expert"][0:E, :], fw["b2"][0:E, :].unsqueeze(1).to_broadcast([E, B, C]),
               start=True, stop=False)
            turn_back(1)
            keep_warm(TAIL_WARM[1])
            centre(1)
            pe.wait_ge(tn_done, 1)
            mm(logit_ps, gw["gate"][:, 0:P], tn[:, 0, :], start=False, stop=False)
            keep_warm(TAIL_WARM[2])
            variance(1)
            keep_warm(TAIL_WARM[3])
            pe.wait_ge(tn_done, 2)
            mm(logit_ps, gw["gate"][:, P:2 * P], tn[:, 1, :], start=False, stop=True).then_inc(logit_done, 1)
            for g in range(GROUPS):
                for h in range(2):
                    last = nc.tensor.transpose(tok_ps[:, g, h, :], tn[:, g, h * HALF:(h + 1) * HALF], ident)
            last.then_inc(tok_done, 1)
            mm(hid_ps, fw["b1"][0:E, :], fw["expert_of"][0:E, :], start=True, stop=False, skip_group_check=True)
            keep_warm(TAIL_WARM[4])
            pe.wait_ge(gprob_done, 1)
            for h in range(2):
                last = nc.tensor.transpose(gpT_ps[:, h, :], gprob[:, h * HALF:(h + 1) * HALF], ident)
            last.then_inc(gpT_done, 1)
            keep_warm(TAIL_WARM[5])
            pe.wait_ge(gpT_copied, 1)
            pe.wait_ge(tok_copied, 1)
            for g in range(GROUPS):
                rows = slice(g * B4 * E, (g + 1) * B4 * E)
                for h in range(2):
                    last = mm(pool_ps[:, rows], tn_tok[:, g, h, :], gprobT[:, h, rows],
                              start=(h == 0), stop=(h == 1))
            last.then_inc(pool_done, 1)
            keep_warm(TAIL_WARM[6])
            pe.wait_ge(pool_copied, 1)
            mm(bank[3][:, 0:P], gw["stack"], pooled[:, :], start=True, stop=True).then_inc(stack_done, 1)
            keep_warm(TAIL_WARM[7])
            pe.wait_ge(stack_copied, 1)
            for j in range(J):
                last = mm(hid_ps[:, j * B * E4:(j + 1) * B * E4], fw["w1"][:, j * HID:(j + 1) * HID],
                          pooled_bd[:, j, :, :].rearrange("p b e -> p (b e)"),
                          start=False, stop=(j == J - 1), skip_group_check=True)
            last.then_inc(hid_done, 1)
            keep_warm(TAIL_WARM[8])
            pe.wait_ge(gelu_done, 1)
            for j in range(J):
                cols = slice(j * B * E4, (j + 1) * B * E4)
                last = mm(eo_ps[:, cols], fw["w2"][:, j * P:(j + 1) * P],
                          hidden[:, j, :, :].rearrange("p b e -> p (b e)"), start=True, stop=True)
            last.then_inc(eo_done, 1)
            keep_warm(TAIL_WARM[9])
            pe.wait_ge(eo_copied, 1)
            mm(tiled_ps, ffn_out[:, :, :, :].rearrange("p b j e -> p (b j e)"), fw["tiled_ident"],
               start=False, stop=True).then_inc(tiled_done, 1)
            keep_warm(TAIL_WARM[10])
            pe.wait_ge(tiled_copied, 1)
            for g in range(GROUPS):
                mm(scat_ps[g], ffn_bd[:, g * P:(g + 1) * P], gprob[:, :],
                   start=True, stop=True).then_inc(scat_done, 1)


def block_diagonal(w):
    r, c = w.shape
    d = np.zeros((B4, r, B4, c), w.dtype)
    for b4 in range(B4):
        d[b4, :, b4, :] = w
    return d.reshape(B4 * r, B4 * c)


def packed(cols, parts):
    where, width = columns(cols)
    a = np.zeros((P, width), np.float32)
    for name, part in parts.items():
        a[0:part.shape[0], where[name]] = part
    return a


def kernel(x, L0_conv_freq_weights, L0_conv_wq, L0_conv_bq, L0_conv_wk, L0_conv_bk, L0_conv_wv, L0_conv_bv,
           L0_conv_wo, L0_conv_bo, L0_ffn_gate_w, L0_ffn_gate_b, L0_ffn_weight1, L0_ffn_weight2):
    import concourse.bacc as bacc
    from concourse.bass_utils import run_bass_kernel_spmd

    f = lambda a: np.asarray(a)
    eye = np.eye(C, dtype=np.float32)
    average = block_diagonal(np.full((C, C), 1.0 / C, np.float32))
    per_channel = lambda a: np.tile(f(a), B4).reshape(P, 1)
    row = np.arange(P)

    gate = np.zeros((P, GROUPS, GROUPS, B4 * E), np.float32)
    for g in range(GROUPS):
        gate[:, g, g, :] = block_diagonal(f(L0_ffn_gate_w).T)
    slot = np.zeros((E4, C, J, B, E4), np.float32)
    for e4 in range(E4):
        slot[e4, :, :, :, e4] = 1.0
    expert = np.zeros((J, E4, J, B, E4), np.float32)
    for e in range(E):
        expert[e // E4, e % E4, e // E4, :, e % E4] = 1.0
    w1, w2 = f(L0_ffn_weight1), f(L0_ffn_weight2)

    arrays = {
        "x": np.ascontiguousarray(f(x)),
        "norm_pack": packed(NORM_COLS, {
            "center": np.eye(P, dtype=np.float32) - average, "average": average,
            "freq": per_channel(L0_conv_freq_weights), "bq": per_channel(L0_conv_bq),
            "bk": per_channel(L0_conv_bk), "bv": per_channel(L0_conv_bv), "bo": per_channel(L0_conv_bo)}),
        "proj_pack": packed(PROJ_COLS, {
            "wq": block_diagonal(f(L0_conv_wq).T), "wk": block_diagonal(f(L0_conv_wk).T),
            "wv": block_diagonal(f(L0_conv_wv)), "wo": block_diagonal(f(L0_conv_wo).T),
            "ident": np.eye(P, dtype=np.float32)}),
        "gate_pack": packed(GATE_COLS, {
            "gate": gate.reshape(P, GROUPS * P), "gate_b": np.tile(f(L0_ffn_gate_b), B).reshape(1, P),
            "own_batch": (row[:, None] // C == (row[None, :] // E) % B4).astype(np.float32),
            "stack": np.tile(eye, (B4, B4)),
            "own_slot": slot.reshape(P, P),
            "own_rows": (row[:, None] // E == np.arange(GROUPS * P)[None, :] // C).astype(np.float32)}),
        "ffn_pack": packed(FFN_COLS, {
            "w1": w1[:, 0:C, :].reshape(J, E4, C, HID).transpose(1, 2, 0, 3).reshape(P, J * HID),
            "w2": w2[:, 0:HID, :].transpose(1, 0, 2).reshape(HID, E * C),
            "b1": w1[:, C, :], "expert_of": expert.reshape(E, P),
            "row_expert": np.tile(np.eye(E, dtype=np.float32), (1, B)),
            "b2": w2[:, HID, :], "tiled_ident": np.tile(eye, (E4, B))}),
    }
    nc = bacc.Bacc("TRN2", target_bir_lowering=False, num_devices=1)
    args = [nc.dram_tensor(n, a.shape, F32, kind="ExternalInput").ap() for n, a in arrays.items()]
    out = nc.dram_tensor("out", (B, C, H, W), F32, kind="ExternalOutput").ap()
    build(nc, *args, out)
    r = run_bass_kernel_spmd(nc, [arrays], core_ids=[0])
    return r.results[0]["out"]
```

```python
from contextlib import ExitStack

import numpy as np

from concourse import mybir

B, C, H, W = 8, 32, 16, 16
N = H * W
GROUPS = 2
B4 = B // GROUPS
P = B4 * C
HALF = N // 2
E, K, HID = 16, 8, 128
E4 = P // C
J = E // E4
START_WARM = 6
LN_C_EPS, LN_T_EPS = 1e-6, 1e-5
SCALE = float(C) ** -0.5
P_SCALE = 4096.0
COMBINED = ((0, 1), (2, 3), (4, 5), (6,), (7,))
SLOTS = 4
PARTS = 3
NOT_A_LOGIT = float(np.finfo(np.float32).min)

F32 = mybir.dt.float32
BF16 = mybir.dt.bfloat16
F16 = mybir.dt.float16
ALU = mybir.AluOpType
ACT = mybir.ActivationFunctionType
AX = mybir.AxisListType

FIRST_COLS = {"center": P, "x0": N}
NORM_COLS = {"x1": N, "average": P, "freq": 1, "bq": 1, "bk": 1, "bv": 1, "bo": 1, "gate_b": 1}
PROJ_COLS = {"wq": P, "wk": P, "wv": P, "wo": P, "ident": P}
GATE_COLS = {"gate": GROUPS * P, "average_rows": GROUPS * P, "own_batch": B, "own_slot": E4, "own_expert": E4,
             "own_rows": B, "stack": P}
FFN_COLS = {"w1": J * HID, "w2": E * C, "b1": HID, "expert_of": P, "b2": C}


def columns(cols):
    at, out = 0, {}
    for name, width in cols.items():
        out[name] = slice(at, at + width)
        at += width
    return out, at


def build(nc, first_pack, norm_pack, proj_pack, gate_pack, ffn_pack, out):
    with ExitStack() as ctx:
        def sb(name, shape, dtype=F32):
            return ctx.enter_context(nc.sbuf_tensor(name, shape, dtype))

        def sem(name):
            return ctx.enter_context(nc.semaphore(name))

        def unpack(name, cols):
            where, width = columns(cols)
            tile = sb(name, [P, width])
            return tile, {k: tile[:, s] for k, s in where.items()}

        first_tile, first = unpack("first_tile", FIRST_COLS)
        norm_tile, nw = unpack("norm_tile", NORM_COLS)
        proj_tile, pw = unpack("proj_tile", PROJ_COLS)
        gate_tile, gw = unpack("gate_tile", GATE_COLS)
        ffn_tile, fw = unpack("ffn_tile", FFN_COLS)
        ident = pw["ident"]

        x_sb = [first["x0"], nw["x1"]]
        center = first["center"]
        eps = sb("eps", [P, 2])
        sq = sb("sq", [P, GROUPS, N])
        log_var = sb("log_var", [P, GROUPS, N])
        rstd = sb("rstd", [P, GROUPS, N])
        y = sb("y", [P, GROUPS, N])
        q = sb("q", [P, GROUPS, N])
        k = sb("k", [P, GROUPS, N])
        wvo = sb("wvo", [P, P])
        bias_out = sb("bias_out", [P, 1])
        x_bias = sb("x_bias", [P, GROUPS, N])
        v = sb("v", [P, GROUPS, 2, B4, C])
        v_rest = sb("v_rest", [P, GROUPS, 2, B4, C])
        v_parts = sb("v_parts", [P, GROUPS, 2, B4, PARTS, C], BF16)
        neg_max = sb("neg_max", [P, B, 2])
        row_sum = sb("row_sum", [P, B, 2])
        row_rcp = sb("row_rcp", [P, B, 2])
        expd = sb("expd", [P, SLOTS, 2, N])
        p_hi = sb("p_hi", [P, SLOTS, 2, N], F16)
        p_lo = sb("p_lo", [P, SLOTS, 2, N], F16)
        attn_sum = sb("attn_sum", [P, B, 2, C])
        attn = sb("attn", [P, GROUPS, 2, B4, C])
        t = sb("t", [P, GROUPS, N])
        tn = sb("tn", [P, GROUPS, N])
        tn_tok = sb("tn_tok", [P, GROUPS, 2, P])
        gate_centred = sb("gate_centred", [P, GROUPS, P])
        rstd_rows = sb("rstd_rows", [P, N])
        log_rows = sb("log_rows", [P, N])
        scaled_logits = sb("scaled_logits", [P, N])
        logits = sb("logits", [P, N])
        top = sb("top", [P, K])
        neg_top = sb("neg_top", [P, 1])
        marked = sb("marked", [P, N])
        chosen = sb("chosen", [P, N])
        gexp = sb("gexp", [P, N])
        gsum = sb("gsum", [P, 1])
        grcp = sb("grcp", [P, 1])
        gprob = sb("gprob", [P, N])
        gprobT = sb("gprobT", [P, 2, P])
        pooled = sb("pooled", [P, P])
        pooled_bd = sb("pooled_bd", [P, J * B, E4])
        hidden = sb("hidden", [P, P])
        ffn_kept = sb("ffn_kept", [P, E4, C])
        ffn_out = sb("ffn_out", [P, C])
        ffn_bd = sb("ffn_bd", [P, GROUPS * P])
        result = sb("result", [P, GROUPS, N])
        warm = sb("warm", [P, 1], BF16)

        bank = [ctx.enter_context(nc.psum_tensor(f"bank{i}", [P, 512], F32)) for i in range(8)]
        xc_ps = [[bank[6][:, 0:HALF], bank[0][:, 0:HALF]], [bank[7][:, 0:N]]]
        var_ps = [[bank[4][:, 0:HALF], bank[1][:, 0:HALF]], [bank[5][:, 0:N]]]
        q_ps = [bank[6][:, 0:N], bank[7][:, 0:N]]
        k_ps = [bank[4][:, 0:N], bank[5][:, 0:N]]
        wvo_ps = bank[3][:, 0:P]
        bias_ps = bank[3][:, P:P + 1]
        v_ps = [bank[6][:, 0:2 * P], bank[7][:, 0:2 * P]]
        score_ps = [bank[i][:, :].rearrange("p (h m) -> p h m", h=2) for i in range(B4)]
        turn_ps = [bank[4 + i][:, :].rearrange("p (h n) -> p h n", h=2) for i in range(2)]
        attn_ps = [b[:, 0:len(u) * 2 * PARTS * C].rearrange("p (b h s) -> p b h s", b=len(u), h=2)
                   for u, b in zip(COMBINED, (bank[6], bank[7], bank[6], bank[7], bank[3]))]
        back_ps = [bank[0][:, 0:N]]
        xc2_ps = [bank[1][:, 0:N]]
        back1_ps = [bank[2][:, 0:HALF], bank[7][:, 0:HALF]]
        xc21_ps = [bank[3][:, 0:HALF], bank[6][:, 0:HALF]]
        var2_ps = [bank[0][:, 0:N], bank[2][:, 0:N]]
        raw_ps = bank[4][:, 0:N]
        var_rows_ps = [bank[5][:, 0:HALF], bank[0][:, 0:HALF]]
        gate_ps = bank[2][:, 0:GROUPS * P]
        tok_ps = [bank[7][:, g * 2 * P:(g + 1) * 2 * P].rearrange("p (h c) -> p h c", h=2) for g in range(GROUPS)]
        gpT_ps = [bank[5][:, 0:P], bank[4][:, 0:P]]
        pool_ps = bank[2][:, 0:P].rearrange("p (j b e) -> p j b e", j=J, b=B)
        stack_ps = bank[3][:, 0:P]
        hid_ps = bank[1][:, 0:P]
        eo_ps = bank[6][:, 0:P]
        scat_ps = [bank[4][:, 0:N], bank[2][:, 0:N]]

        first_in, norm_in, proj_in = sem("first_in"), sem("norm_in"), sem("proj_in")
        gate_in, ffn_in = sem("gate_in"), sem("ffn_in")
        ready = sem("ready")
        xc_done, sq_done, var_done = sem("xc_done"), sem("sq_done"), sem("var_done")
        log_done, rstd_done, y_done = sem("log_done"), sem("rstd_done"), sem("y_done")
        wvo_done, wvo_copied = sem("wvo_done"), sem("wvo_copied")
        qp_done, kp_done, vp_done = sem("qp_done"), sem("kp_done"), sem("vp_done")
        q_done, k_done, v_done = sem("q_done"), sem("k_done"), sem("v_done")
        score_done, max_done, exp_done = sem("score_done"), sem("max_done"), sem("exp_done")
        rcp_done, bias_done = sem("rcp_done"), sem("bias_done")
        turn_done, hi_done, lo_done, attn_done = sem("turn_done"), sem("hi_done"), sem("lo_done"), sem("attn_done")
        split_step, split_done, x_bias_done = sem("split_step"), sem("split_done"), sem("x_bias_done")
        summed, scaled, pairs_scaled, back_done = sem("summed"), sem("scaled"), sem("pairs_scaled"), sem("back_done")
        t_done, xc2_done, sq2_done, var2_done = sem("t_done"), sem("xc2_done"), sem("sq2_done"), sem("var2_done")
        log2_done, rstd2_done, tn_done = sem("log2_done"), sem("rstd2_done"), sem("tn_done")
        raw_done, var_rows_done, log_rows_done = sem("raw_done"), sem("var_rows_done"), sem("log_rows_done")
        rstd_rows_done, scaled_logits_done = sem("rstd_rows_done"), sem("scaled_logits_done")
        logit_done = sem("logit_done")
        gate_done, gate_copied = sem("gate_done"), sem("gate_copied")
        top_done, neg_done = sem("top_done"), sem("neg_done")
        mark_done, chosen_done, gexp_done = sem("mark_done"), sem("chosen_done"), sem("gexp_done")
        grcp_done, gprob_done = sem("grcp_done"), sem("gprob_done")
        tok_done, tok_copied, gpT_done = sem("tok_done"), sem("tok_copied"), sem("gpT_done")
        gpT_copied, pool_done, pool_copied = sem("gpT_copied"), sem("pool_done"), sem("pool_copied")
        stack_done, stack_copied = sem("stack_done"), sem("stack_copied")
        hid_done, gelu_done, eo_done, kept_done = sem("hid_done"), sem("gelu_done"), sem("eo_done"), sem("kept_done")
        ffn_out_done, ffn_bd_done, scat_done = sem("ffn_out_done"), sem("ffn_bd_done"), sem("scat_done")
        result1_done, result0_done, stored = sem("result1_done"), sem("result0_done"), sem("stored")

        out_cm = out.rearrange("(g b) c h w -> g (b c) (h w)", g=GROUPS)

        halves = [slice(h * HALF, (h + 1) * HALF) for h in range(2)]

        block = ctx.enter_context(nc.Block())

        @block.sync
        def _(sp):
            sp.dma_start(first_tile[:, :], first_pack).then_inc(first_in, 16)
            sp.dma_start(proj_tile[:, :], proj_pack).then_inc(proj_in, 16)
            sp.dma_start(gate_tile[:, :], gate_pack).then_inc(gate_in, 16)
            sp.dma_start(ffn_tile[:, :], ffn_pack).then_inc(ffn_in, 16)
            sp.wait_ge(result1_done, 1)
            sp.dma_start(out_cm[1], result[:, 1, :]).then_inc(stored, 16)
            sp.wait_ge(stored, 16 * GROUPS)

        @block.gpsimd
        def _(pool):
            def step(ins, n):
                ins.then_inc(split_step, 1)
                pool.wait_ge(split_step, n)

            def divide(u):
                batches = slice(COMBINED[u][0], COMBINED[u][-1] + 1)
                g, b4s = batches.start // B4, slice(batches.start % B4, batches.start % B4 + len(COMBINED[u]))
                pool.wait_ge(summed, u + 1)
                pool.wait_ge(rcp_done, u + 1)
                nc.gpsimd.tensor_tensor(attn[:, g, :, b4s, :].rearrange("p h b c -> p b h c"), attn_sum[:, batches],
                                        row_rcp[:, batches, :].unsqueeze(3).to_broadcast([P, len(COMBINED[u]), 2, C]),
                                        ALU.mult).then_inc(pairs_scaled, 1)

            for g in range(GROUPS):
                pool.wait_ge(v_done, g + 1)
                part = [v_parts[:, g, :, :, s, :] for s in range(PARTS)]
                step(nc.gpsimd.tensor_tensor(v_rest[:, g], v[:, g], part[0], ALU.subtract), 2 * g + 1)
                step(nc.gpsimd.tensor_copy(part[1], v_rest[:, g]), 2 * g + 2)
                nc.gpsimd.tensor_tensor(part[2], v_rest[:, g], part[1], ALU.subtract).then_inc(split_done, 1)

            divide(0)
            pool.wait_ge(bias_done, 1)
            pool.wait_ge(first_in, 16)
            pool.wait_ge(norm_in, 16)
            for g in range(GROUPS):
                nc.gpsimd.tensor_scalar(x_bias[:, g, :], x_sb[g], bias_out[:, :], 1.0, ALU.add,
                                        ALU.mult).then_inc(x_bias_done, 1)

            divide(1)
            divide(2)

        @block.scalar
        def _(act):
            act.dma_start(norm_tile[:, :], norm_pack).then_inc(norm_in, 16)
            nc.scalar.preload_act_table_set("natural_log_exp_and_others")

            act.wait_ge(ready, 3)

            def square_x(g):
                for i, cols in enumerate(halves if g == 0 else [slice(0, N)]):
                    act.wait_ge(xc_done, 2 * g + i + 1)
                    nc.scalar.activation(sq[:, g, cols], xc_ps[g][i], ACT.Square).then_inc(sq_done, 1)

            def inverse_deviation_x(g):
                cuts = halves if g == 0 else [slice(0, N)]
                for i, cols in enumerate(cuts):
                    act.wait_ge(var_done, 2 * g + i + 1)
                    nc.scalar.activation(log_var[:, g, cols], var_ps[g][i], ACT.Ln,
                                         bias=eps[:, 0:1]).then_inc(log_done, 1)
                for i, cols in enumerate(cuts):
                    act.wait_ge(log_done, 2 * g + i + 1)
                    nc.scalar.activation(rstd[:, g, cols], log_var[:, g, cols], ACT.Exp,
                                         scale=-0.5).then_inc(rstd_done, 1)

            def copy_gate():
                act.wait_ge(gate_done, 1)
                nc.scalar.copy(gate_centred[:, :, :].rearrange("p g r -> p (g r)"), gate_ps).then_inc(gate_copied, 1)

            def keys(g):
                act.wait_ge(kp_done, g + 1)
                nc.scalar.activation(k[:, g, :], k_ps[g], ACT.Identity, bias=nw["bk"]).then_inc(k_done, 1)

            def values(g):
                act.wait_ge(vp_done, g + 1)
                nc.scalar.copy(v_parts[:, g, :, :, 0, :], v_ps[g].rearrange("p (h b c) -> p h b c", h=2, b=B4))
                nc.scalar.copy(v[:, g].rearrange("p h b c -> p (h b c)"), v_ps[g]).then_inc(v_done, 1)

            def exponentials(b):
                act.wait_ge(max_done, b + 1)
                if b >= SLOTS:
                    act.wait_ge(turn_done, b - SLOTS + 1)
                for h in range(2):
                    nc.scalar.activation(expd[:, b % SLOTS, h, :], score_ps[b % B4][:, h, :], ACT.Exp,
                                         bias=neg_max[:, b, h:h + 1],
                                         accum_out=row_sum[:, b, h:h + 1]).then_inc(exp_done, 1)

            def high_part(b):
                act.wait_ge(turn_done, b + 1)
                if b >= SLOTS:
                    act.wait_ge(attn_done, b - SLOTS + 1)
                nc.scalar.activation(p_hi[:, b % SLOTS], turn_ps[b % 2], ACT.Identity,
                                     scale=P_SCALE).then_inc(hi_done, 1)

            def square(g):
                if g == 0:
                    act.wait_ge(xc2_done, 1)
                    nc.scalar.activation(sq[:, 0, :], xc2_ps[0], ACT.Square).then_inc(sq2_done, 1)
                else:
                    for h in range(2):
                        act.wait_ge(xc2_done, 2 + h)
                        nc.scalar.activation(sq[:, 1, h * HALF:(h + 1) * HALF], xc21_ps[h],
                                             ACT.Square).then_inc(sq2_done, 1)

            def log_variance(g):
                act.wait_ge(var2_done, g + 1)
                nc.scalar.activation(log_var[:, g, :], var2_ps[g], ACT.Ln, bias=eps[:, 1:2]).then_inc(log2_done, 1)

            def inverse_deviation(g):
                act.wait_ge(log2_done, g + 1)
                nc.scalar.activation(rstd[:, g, :], log_var[:, g, :], ACT.Exp, scale=-0.5).then_inc(rstd2_done, 1)

            def rows_deviation():
                for h in range(2):
                    act.wait_ge(var_rows_done, h + 1)
                    nc.scalar.activation(log_rows[:, halves[h]], var_rows_ps[h], ACT.Ln,
                                         bias=eps[:, 1:2]).then_inc(log_rows_done, 1)
                for h in range(2):
                    act.wait_ge(log_rows_done, h + 1)
                    nc.scalar.activation(rstd_rows[:, halves[h]], log_rows[:, halves[h]], ACT.Exp,
                                         scale=-0.5).then_inc(rstd_rows_done, 1)

            square_x(0)
            inverse_deviation_x(0)
            square_x(1)
            keys(0)
            inverse_deviation_x(1)
            copy_gate()
            exponentials(0)
            values(0)
            exponentials(1)
            keys(1)
            high_part(0)
            exponentials(2)
            high_part(1)
            exponentials(3)
            high_part(2)
            values(1)
            exponentials(4)
            high_part(3)
            exponentials(5)
            high_part(4)
            exponentials(6)
            high_part(5)
            exponentials(7)
            high_part(6)
            high_part(7)
            square(0)
            log_variance(0)
            inverse_deviation(0)
            square(1)
            rows_deviation()
            log_variance(1)

            act.wait_ge(scaled_logits_done, 2)
            nc.scalar.activation(logits[:, :], scaled_logits[:, :], ACT.Identity,
                                 bias=nw["gate_b"]).then_inc(logit_done, 1)
            inverse_deviation(1)
            act.wait_ge(logit_done, 1)
            act.wait_ge(neg_done, 1)
            nc.scalar.activation(gexp[:, :], logits[:, :], ACT.Exp, bias=neg_top[:, :],
                                 accum_out=gsum[:, :]).then_inc(gexp_done, 1)
            for g in range(GROUPS):
                act.wait_ge(tok_done, g + 1)
                nc.scalar.copy(tn_tok[:, g], tok_ps[g]).then_inc(tok_copied, 1)
            nc.scalar.preload_act_table(ACT.Gelu)
            act.wait_ge(hid_done, 1)
            nc.scalar.activation(hidden[:, :], hid_ps,
                                 ACT.Gelu).then_inc(gelu_done, 1)
            act.wait_ge(scat_done, 1)
            nc.scalar.copy(result[:, 0, :], scat_ps[0]).then_inc(result0_done, 1)
            act.wait_ge(result0_done, 1)
            act.dma_start(out_cm[0], result[:, 0, :]).then_inc(stored, 16)

        @block.vector
        def _(dve):
            nc.vector.memset(warm[:, :], 0.0).then_inc(ready, 1)
            nc.vector.memset(eps[:, 0:1], LN_C_EPS).then_inc(ready, 1)
            nc.vector.memset(eps[:, 1:2], LN_T_EPS).then_inc(ready, 1)
            def copy_wvo():
                dve.wait_ge(wvo_done, 1)
                nc.vector.tensor_copy(wvo[:, :], wvo_ps).then_inc(wvo_copied, 1)

            def output_bias():
                dve.wait_ge(wvo_done, 1)
                dve.wait_ge(norm_in, 16)
                nc.vector.tensor_scalar(bias_out[:, :], bias_ps, nw["bo"], None, ALU.add).then_inc(bias_done, 1)

            def layer_norm(g):
                dve.wait_ge(norm_in, 16)
                for i, cols in enumerate(halves if g == 0 else [slice(0, N)]):
                    dve.wait_ge(rstd_done, 2 * g + i + 1)
                    nc.vector.scalar_tensor_tensor(y[:, g, cols], xc_ps[g][i], nw["freq"], rstd[:, g, cols],
                                                   ALU.mult, ALU.mult).then_inc(y_done, 1)

            def queries(g):
                dve.wait_ge(qp_done, g + 1)
                for cols in halves if g == 0 else [slice(0, N)]:
                    nc.vector.tensor_scalar(q[:, g, cols], q_ps[g][:, cols], nw["bq"], SCALE, ALU.add,
                                            ALU.mult).then_inc(q_done, 1)

            def row_maxima(b):
                dve.wait_ge(score_done, b + 1)
                nc.vector.tensor_reduce(neg_max[:, b, :], score_ps[b % B4], AX.X, ALU.max,
                                        negate=True).then_inc(max_done, 1)

            def low_part(b):
                dve.wait_ge(hi_done, b + 1)
                nc.vector.scalar_tensor_tensor(p_lo[:, b % SLOTS].rearrange("p m n -> p (m n)"),
                                               turn_ps[b % 2].rearrange("p m n -> p (m n)"), P_SCALE,
                                               p_hi[:, b % SLOTS].rearrange("p m n -> p (m n)"),
                                               ALU.mult, ALU.subtract).then_inc(lo_done, 1)

            def reciprocals(u):
                batches = slice(COMBINED[u][0], COMBINED[u][-1] + 1)
                dve.wait_ge(exp_done, 2 * batches.stop)
                nc.vector.reciprocal(row_rcp[:, batches, :], row_sum[:, batches, :]).then_inc(rcp_done, 1)

            def combine(u):
                batches = slice(COMBINED[u][0], COMBINED[u][-1] + 1)
                dve.wait_ge(attn_done, batches.stop)
                nc.vector.tensor_reduce(attn_sum[:, batches].rearrange("p b h c -> p (b h) c"),
                                        attn_ps[u].rearrange("p b h (s c) -> p (b h) c s", s=PARTS),
                                        AX.X, ALU.add).then_inc(summed, 1)

            def divide(u):
                batches = slice(COMBINED[u][0], COMBINED[u][-1] + 1)
                g, b4s = batches.start // B4, slice(batches.start % B4, batches.start % B4 + len(COMBINED[u]))
                dve.wait_ge(summed, u + 1)
                dve.wait_ge(rcp_done, u + 1)
                nc.vector.tensor_tensor(attn[:, g, :, b4s, :].rearrange("p h b c -> p b h c"), attn_sum[:, batches],
                                        row_rcp[:, batches, :].unsqueeze(3).to_broadcast([P, len(COMBINED[u]), 2, C]),
                                        ALU.mult).then_inc(scaled, 1)

            def add_residual(g):
                dve.wait_ge(x_bias_done, g + 1)
                if g == 0:
                    dve.wait_ge(back_done, 1)
                    nc.vector.scalar_tensor_tensor(t[:, 0, :], back_ps[0], 1.0 / P_SCALE, x_bias[:, 0, :],
                                                   ALU.mult, ALU.add).then_inc(t_done, 1)
                else:
                    for h in range(2):
                        half = slice(h * HALF, (h + 1) * HALF)
                        dve.wait_ge(back_done, 2 + h)
                        nc.vector.scalar_tensor_tensor(t[:, 1, half], back1_ps[h], 1.0 / P_SCALE, x_bias[:, 1, half],
                                                       ALU.mult, ALU.add).then_inc(t_done, 1)

            def normalise():
                dve.wait_ge(rstd2_done, 1)
                nc.vector.tensor_tensor(tn[:, 0, :], xc2_ps[0], rstd[:, 0, :], ALU.mult).then_inc(tn_done, 1)

            def normalise_half(h):
                half = slice(h * HALF, (h + 1) * HALF)
                dve.wait_ge(rstd2_done, 2)
                nc.vector.tensor_tensor(tn[:, 1, half], xc21_ps[h], rstd[:, 1, half], ALU.mult).then_inc(tn_done, 1)

            layer_norm(0)
            queries(0)
            copy_wvo()
            row_maxima(0)
            layer_norm(1)
            output_bias()
            row_maxima(1)
            queries(1)
            row_maxima(2)
            row_maxima(3)
            reciprocals(0)
            low_part(0)
            low_part(1)
            row_maxima(4)
            low_part(2)
            row_maxima(5)
            combine(0)
            low_part(3)
            row_maxima(6)
            reciprocals(1)
            reciprocals(2)
            low_part(4)
            row_maxima(7)
            combine(1)
            low_part(5)
            reciprocals(3)
            reciprocals(4)
            low_part(6)
            add_residual(0)
            low_part(7)
            combine(2)
            combine(3)
            combine(4)
            divide(3)
            divide(4)
            add_residual(1)
            normalise()

            dve.wait_ge(raw_done, 1)
            for h in range(2):
                half = slice(h * HALF, (h + 1) * HALF)
                dve.wait_ge(rstd_rows_done, h + 1)
                nc.vector.tensor_tensor(scaled_logits[:, half], raw_ps[:, half], rstd_rows[:, half],
                                        ALU.mult).then_inc(scaled_logits_done, 1)
            dve.wait_ge(scaled_logits_done, 2)
            nc.vector.max(top[:, :], scaled_logits[:, :]).then_inc(top_done, 1)
            dve.wait_ge(top_done, 1)
            nc.vector.tensor_scalar(neg_top[:, :], top[:, 0:1], nw["gate_b"], -1.0, ALU.add,
                                    ALU.mult).then_inc(neg_done, 1)
            nc.vector.match_replace(marked[:, :], top[:, :], scaled_logits[:, :], NOT_A_LOGIT).then_inc(mark_done, 1)
            normalise_half(0)
            dve.wait_ge(mark_done, 1)
            nc.vector.tensor_scalar(chosen[:, :], marked[:, :], NOT_A_LOGIT, None,
                                    ALU.is_equal).then_inc(chosen_done, 1)
            dve.wait_ge(gexp_done, 1)
            nc.vector.reciprocal(grcp[:, :], gsum[:, :]).then_inc(grcp_done, 1)
            normalise_half(1)
            dve.wait_ge(chosen_done, 1)
            dve.wait_ge(grcp_done, 1)
            for h in range(2):
                half = slice(h * HALF, (h + 1) * HALF)
                nc.vector.scalar_tensor_tensor(gprob[:, half], gexp[:, half], grcp[:, :], chosen[:, half],
                                               ALU.mult, ALU.mult).then_inc(gprob_done, 1)
            for h in range(2):
                dve.wait_ge(gpT_done, h + 1)
                nc.vector.tensor_copy(gprobT[:, h, :], gpT_ps[h]).then_inc(gpT_copied, 1)
            dve.wait_ge(pool_done, 1)
            nc.vector.tensor_tensor(pooled[:, :].rearrange("p (j b e) -> p j b e", j=J, b=B), pool_ps,
                                    gw["own_batch"].unsqueeze(1).unsqueeze(3).to_broadcast([P, J, B, E4]),
                                    ALU.mult).then_inc(pool_copied, 1)
            dve.wait_ge(stack_done, 1)
            nc.vector.tensor_tensor(pooled_bd[:, :, :], stack_ps.rearrange("p (r e) -> p r e", e=E4),
                                    gw["own_slot"].unsqueeze(1).to_broadcast([P, J * B, E4]),
                                    ALU.mult).then_inc(stack_copied, 1)
            dve.wait_ge(eo_done, 1)
            nc.vector.tensor_tensor(ffn_kept[:, :, :], eo_ps.rearrange("p (e c) -> p e c", e=E4),
                                    gw["own_expert"].unsqueeze(2).to_broadcast([P, E4, C]),
                                    ALU.mult).then_inc(kept_done, 1)
            dve.wait_ge(kept_done, 1)
            nc.vector.tensor_reduce(ffn_out[:, :], ffn_kept[:, :, :].rearrange("p e c -> p c e"), AX.X,
                                    ALU.add).then_inc(ffn_out_done, 1)
            dve.wait_ge(ffn_out_done, 1)
            for g in range(GROUPS):
                nc.vector.tensor_tensor(ffn_bd[:, g * P:(g + 1) * P].rearrange("p (b c) -> p b c", b=B4),
                                        ffn_out[:, :].unsqueeze(1).to_broadcast([P, B4, C]),
                                        gw["own_rows"][:, g * B4:(g + 1) * B4].unsqueeze(2).to_broadcast([P, B4, C]),
                                        ALU.mult).then_inc(ffn_bd_done, 1)
            dve.wait_ge(scat_done, 2)
            nc.vector.tensor_copy(result[:, 1, :], scat_ps[1]).then_inc(result1_done, 1)

        @block.tensor
        def _(pe):
            mm = nc.tensor.matmul

            def keep_warm(n, spare):
                for _ in range(n):
                    mm(spare[:, :], warm[:, :].to_broadcast([P, P]), warm[:, :].to_broadcast([P, 512]),
                       start=True, stop=True)

            pe.wait_ge(ready, 1)
            keep_warm(START_WARM, bank[7])

            def centre_x0():
                pe.wait_ge(first_in, 16)
                for i, cols in enumerate(halves):
                    mm(xc_ps[0][i], center, x_sb[0][:, cols], start=True, stop=True).then_inc(xc_done, 1)

            def centre_x1(h):
                pe.wait_ge(norm_in, 16)
                last = mm(xc_ps[1][0][:, halves[h]], center, x_sb[1][:, halves[h]], start=True, stop=True)
                if h == 1:
                    last.then_inc(xc_done, 1)

            def variance_x(g):
                pe.wait_ge(norm_in, 16)
                for i, cols in enumerate(halves if g == 0 else [slice(0, N)]):
                    pe.wait_ge(sq_done, 2 * g + i + 1)
                    mm(var_ps[g][i], nw["average"], sq[:, g, cols], start=True, stop=True).then_inc(var_done, 1)

            def fold_values():
                pe.wait_ge(proj_in, 16)
                pe.wait_ge(norm_in, 16)
                mm(bias_ps, pw["wo"], nw["bv"], start=True, stop=True)
                mm(wvo_ps, pw["wv"], pw["wo"], start=True, stop=True).then_inc(wvo_done, 1)

            def fold_gate():
                pe.wait_ge(gate_in, 16)
                mm(gate_ps, center, gw["gate"], start=True, stop=True).then_inc(gate_done, 1)

            def project_q(g):
                pe.wait_ge(proj_in, 16)
                pe.wait_ge(y_done, 2 + g)
                mm(q_ps[g], pw["wq"], y[:, g, :], start=True, stop=True).then_inc(qp_done, 1)

            def project_k(g):
                pe.wait_ge(proj_in, 16)
                if g == 1:
                    pe.wait_ge(y_done, 3)
                for h, cols in enumerate(halves):
                    if g == 0:
                        pe.wait_ge(y_done, h + 1)
                    last = mm(k_ps[g][:, cols], pw["wk"], y[:, g, cols], start=True, stop=True)
                last.then_inc(kp_done, 1)

            def values(g):
                pe.wait_ge(wvo_copied, 1)
                pe.wait_ge(y_done, 2 + g)
                pe.wait_ge(q_done, 2 + g)
                for h in range(2):
                    last = mm(v_ps[g][:, h * P:(h + 1) * P], y[:, g, h * HALF:(h + 1) * HALF], wvo[:, :],
                              start=True, stop=True)
                last.then_inc(vp_done, 1)

            def scores(b):
                g, b4 = b // B4, b % B4
                pe.wait_ge(k_done, g + 1)
                if b == 2:
                    pe.wait_ge(gate_copied, 1)
                if b == 3:
                    pe.wait_ge(wvo_copied, 1)
                    pe.wait_ge(bias_done, 1)
                if b >= B4:
                    pe.wait_ge(exp_done, 2 * (b4 + 1))
                rows = slice(C * b4, C * (b4 + 1))
                for h in range(2):
                    pe.wait_ge(q_done, h + 1 if g == 0 else 3)
                    last = mm(score_ps[b4][:, h, :], q[rows, g, h * HALF:(h + 1) * HALF], k[rows, g, :],
                              start=True, stop=True)
                last.then_inc(score_done, 1)

            def turn(b):
                pe.wait_ge(exp_done, 2 * (b + 1))
                if b == 1:
                    pe.wait_ge(k_done, 2)
                if b >= 2:
                    pe.wait_ge(lo_done, b - 1)
                for h in range(2):
                    for m in range(2):
                        last = nc.tensor.transpose(turn_ps[b % 2][:, m, h * HALF:(h + 1) * HALF],
                                                   expd[:, b % SLOTS, h, m * HALF:(m + 1) * HALF], ident)
                last.then_inc(turn_done, 1)

            def attend(b):
                g, b4 = b // B4, b % B4
                u = [b in batches for batches in COMBINED].index(True)
                if b % B4 == 0:
                    pe.wait_ge(split_done, g + 1)
                if b == 2:
                    pe.wait_ge(v_done, 2)
                if b in (4, 6):
                    pe.wait_ge(summed, u - 1)
                if b == 7:
                    pe.wait_ge(exp_done, 2 * B)
                pe.wait_ge(lo_done, b + 1)
                for h in range(2):
                    terms = [(part, m) for m in range(2) for part in (p_hi, p_lo)]
                    for i, (part, m) in enumerate(terms):
                        last = mm(attn_ps[u][:, b - COMBINED[u][0], h, :],
                                  part[:, b % SLOTS, m, h * HALF:(h + 1) * HALF],
                                  v_parts[:, g, m, b4].rearrange("p s c -> p (s c)"),
                                  start=(i == 0), stop=(i == len(terms) - 1))
                last.then_inc(attn_done, 1)

            def turn_back(g):
                pe.wait_ge(pairs_scaled, 2 if g == 0 else 3)
                if g == 1:
                    pe.wait_ge(scaled, 2)
                pe.wait_ge(exp_done, 2 * B4 + 2 * (1 if g == 0 else 3))
                for h in range(2):
                    out_ps = back_ps[0][:, h * HALF:(h + 1) * HALF] if g == 0 else back1_ps[h]
                    last = nc.tensor.transpose(out_ps, attn[:, g, h].rearrange("p b c -> p (b c)"), ident)
                    if g == 1 or h == 1:
                        last.then_inc(back_done, 1)

            def centre(g):
                pe.wait_ge(exp_done, 2 * B4 + 2 * (2 if g == 0 else 4))
                if g == 0:
                    pe.wait_ge(t_done, 1)
                    mm(xc2_ps[0], center, t[:, 0, :], start=True, stop=True).then_inc(xc2_done, 1)
                else:
                    for h in range(2):
                        pe.wait_ge(t_done, 2 + h)
                        mm(xc21_ps[h], center, t[:, 1, h * HALF:(h + 1) * HALF],
                           start=True, stop=True).then_inc(xc2_done, 1)

            def variance(g):
                pe.wait_ge(sq2_done, 1 if g == 0 else 3)
                pe.wait_ge(t_done, 1 if g == 0 else 3)
                mm(var2_ps[g], nw["average"], sq[:, g, :], start=True, stop=True).then_inc(var2_done, 1)

            def raw_logits(g):
                pe.wait_ge(t_done, 1 if g == 0 else 3)
                pe.wait_ge(lo_done, B - 1)
                last = mm(raw_ps, gate_centred[:, g, :], t[:, g, :], start=(g == 0), stop=(g == 1))
                if g == 1:
                    last.then_inc(raw_done, 1)

            def rows_variance(g):
                for h in range(2):
                    pe.wait_ge(sq2_done, 1 if g == 0 else 2 + h)
                    pe.wait_ge(lo_done, B)
                    pe.wait_ge(log2_done, 1)
                    last = mm(var_rows_ps[h], gw["average_rows"][:, g * P:(g + 1) * P],
                              sq[:, g, h * HALF:(h + 1) * HALF], start=(g == 0), stop=(g == 1))
                    if g == 1:
                        last.then_inc(var_rows_done, 1)

            def ffn_biases():
                pe.wait_ge(ffn_in, 16)
                pe.wait_ge(tn_done, 3)
                mm(eo_ps, fw["expert_of"][0:E, :], fw["b2"][0:E, :].unsqueeze(1).to_broadcast([E, E4, C]),
                   start=True, stop=False, skip_group_check=True)

            def hidden_biases():
                pe.wait_ge(ffn_in, 16)
                pe.wait_ge(tn_done, 1)
                mm(hid_ps, fw["b1"][0:E, :], fw["expert_of"][0:E, :], start=True, stop=False, skip_group_check=True)

            def turn_gate():
                for h in range(2):
                    pe.wait_ge(gprob_done, h + 1)
                    nc.tensor.transpose(gpT_ps[h], gprob[:, h * HALF:(h + 1) * HALF], ident).then_inc(gpT_done, 1)

            def tokens(g):
                pe.wait_ge(tn_done, 1 if g == 0 else 3)
                pe.wait_ge(t_done, 3)
                if g == 1:
                    pe.wait_ge(tok_copied, 1)
                for h in range(2):
                    last = nc.tensor.transpose(tok_ps[g][:, h, :], tn[:, g, h * HALF:(h + 1) * HALF], ident)
                last.then_inc(tok_done, 1)

            centre_x0()
            centre_x1(0)
            variance_x(0)
            centre_x1(1)
            fold_values()
            project_k(0)
            project_q(0)
            fold_gate()
            variance_x(1)
            scores(0)
            values(0)
            scores(1)
            scores(2)
            project_q(1)
            project_k(1)
            turn(0)
            scores(3)
            values(1)
            turn(1)
            scores(4)
            turn(2)
            attend(0)
            attend(1)
            scores(5)
            turn(3)
            scores(6)
            turn(4)
            scores(7)
            turn(5)
            attend(2)
            attend(3)
            turn(6)
            attend(4)
            turn(7)
            turn_back(0)
            attend(5)
            attend(6)
            centre(0)
            pe.wait_ge(exp_done, 2 * B)
            attend(7)
            variance(0)
            turn_back(1)
            raw_logits(0)
            centre(1)
            rows_variance(0)
            rows_variance(1)
            raw_logits(1)
            variance(1)
            hidden_biases()
            tokens(0)
            pe.wait_ge(log_rows_done, 2)
            keep_warm(4, bank[0])
            tokens(1)
            turn_gate()
            keep_warm(1, bank[0])
            ffn_biases()

            def residual(g):
                mm(scat_ps[g], ident, t[:, g, :], start=True, stop=False)

            for g in range(GROUPS):
                own = slice(g * B4, (g + 1) * B4)
                for h in range(2):
                    if h == 0:
                        pe.wait_ge(tok_copied, g + 1)
                    if g == 0:
                        pe.wait_ge(gpT_copied, h + 1)
                    last = mm(pool_ps[:, :, own, :], tn_tok[:, g, h, :],
                              gprobT[:, h, :].rearrange("p (j b e) -> p j b e", j=J, b=B)[:, :, own, :],
                              start=(h == 0), stop=(h == 1), skip_group_check=True)
            last.then_inc(pool_done, 1)
            residual(0)
            pe.wait_ge(pool_copied, 1)
            mm(stack_ps, gw["stack"], pooled[:, :], start=True, stop=True).then_inc(stack_done, 1)
            residual(1)
            keep_warm(1, bank[0])
            pe.wait_ge(stack_copied, 1)
            for j in range(J):
                cols = slice(j * B * E4, (j + 1) * B * E4)
                last = mm(hid_ps[:, cols], fw["w1"][:, j * HID:(j + 1) * HID],
                          pooled_bd[:, j * B:(j + 1) * B, :].rearrange("p b e -> p (b e)"),
                          start=False, stop=(j == J - 1), skip_group_check=True)
            last.then_inc(hid_done, 1)
            keep_warm(1, bank[0])
            pe.wait_ge(gelu_done, 1)
            for j in range(J):
                rows = slice(j * B * E4, (j + 1) * B * E4)
                last = mm(eo_ps[rows, :], hidden[:, rows], fw["w2"][:, j * P:(j + 1) * P],
                          start=False, stop=True, skip_group_check=True, tile_position=(0, j * C))
            last.then_inc(eo_done, 1)
            keep_warm(2, bank[0])
            for g in range(GROUPS):
                pe.wait_ge(ffn_bd_done, g + 1)
                mm(scat_ps[g], ffn_bd[:, g * P:(g + 1) * P], gprob[:, :],
                   start=False, stop=True).then_inc(scat_done, 1)


def block_diagonal(w):
    r, c = w.shape
    d = np.zeros((B4, r, B4, c), w.dtype)
    for b4 in range(B4):
        d[b4, :, b4, :] = w
    return d.reshape(B4 * r, B4 * c)


def packed(cols, parts):
    where, width = columns(cols)
    a = np.zeros((P, width), np.float32)
    for name, part in parts.items():
        a[0:part.shape[0], where[name]] = part
    return a


def kernel(x, L0_conv_freq_weights, L0_conv_wq, L0_conv_bq, L0_conv_wk, L0_conv_bk, L0_conv_wv, L0_conv_bv,
           L0_conv_wo, L0_conv_bo, L0_ffn_gate_w, L0_ffn_gate_b, L0_ffn_weight1, L0_ffn_weight2):
    import concourse.bacc as bacc
    from concourse.bass_utils import run_bass_kernel_spmd

    f = lambda a: np.asarray(a)
    eye = np.eye(C, dtype=np.float32)
    average = block_diagonal(np.full((C, C), 1.0 / C, np.float32))
    per_channel = lambda a: np.tile(f(a), B4).reshape(P, 1)
    row = np.arange(P)

    rows_j, rows_b, rows_e4 = (a.reshape(P) for a in np.indices((J, B, E4)))
    gate_w = f(L0_ffn_gate_w).reshape(J, E4, C)
    gate = np.zeros((B4, C, GROUPS, J, B, E4), np.float32)
    average_rows = np.zeros((B4, C, GROUPS, J, B, E4), np.float32)
    for b in range(B):
        gate[b % B4, :, b // B4, :, b, :] = gate_w.transpose(2, 0, 1)
        average_rows[b % B4, :, b // B4, :, b, :] = 1.0 / C
    expert_of = (np.arange(E)[:, None] == (E4 * rows_j + rows_e4)[None, :]).astype(np.float32)
    w1, w2 = f(L0_ffn_weight1), f(L0_ffn_weight2)
    x_cm = f(x).reshape(GROUPS, P, N)

    arrays = {
        "first_pack": packed(FIRST_COLS, {"center": np.eye(P, dtype=np.float32) - average, "x0": x_cm[0]}),
        "norm_pack": packed(NORM_COLS, {
            "x1": x_cm[1], "average": average,
            "freq": per_channel(L0_conv_freq_weights), "bq": per_channel(L0_conv_bq),
            "bk": per_channel(L0_conv_bk), "bv": per_channel(L0_conv_bv), "bo": per_channel(L0_conv_bo),
            "gate_b": f(L0_ffn_gate_b)[E4 * rows_j + rows_e4].reshape(P, 1)}),
        "proj_pack": packed(PROJ_COLS, {
            "wq": block_diagonal(f(L0_conv_wq).T), "wk": block_diagonal(f(L0_conv_wk).T),
            "wv": block_diagonal(f(L0_conv_wv)), "wo": block_diagonal(f(L0_conv_wo).T),
            "ident": np.eye(P, dtype=np.float32)}),
        "gate_pack": packed(GATE_COLS, {
            "gate": gate.reshape(P, GROUPS * P), "average_rows": average_rows.reshape(P, GROUPS * P),
            "own_batch": (row[:, None] // C == np.arange(B)[None, :] % B4).astype(np.float32),
            "own_slot": (row[:, None] // C == np.arange(E4)[None, :]).astype(np.float32),
            "own_expert": (rows_e4[:, None] == np.arange(E4)[None, :]).astype(np.float32),
            "own_rows": (rows_b[:, None] == np.arange(B)[None, :]).astype(np.float32),
            "stack": np.tile(eye, (B4, B4))}),
        "ffn_pack": packed(FFN_COLS, {
            "w1": w1[:, 0:C, :].reshape(J, E4, C, HID).transpose(1, 2, 0, 3).reshape(P, J * HID),
            "w2": w2[:, 0:HID, :].transpose(1, 0, 2).reshape(HID, E * C),
            "b1": w1[:, C, :], "expert_of": expert_of, "b2": w2[:, HID, :]}),
    }
    nc = bacc.Bacc("TRN2", target_bir_lowering=False, num_devices=1)
    args = [nc.dram_tensor(n, a.shape, F32, kind="ExternalInput").ap() for n, a in arrays.items()]
    out = nc.dram_tensor("out", (B, C, H, W), F32, kind="ExternalOutput").ap()
    build(nc, *args, out)
    r = run_bass_kernel_spmd(nc, [arrays], core_ids=[0])
    return r.results[0]["out"]
```
